# Optimizing a Trainium2 kernel written in Bass

```python
import numpy as np
import jax
import jax.numpy as jnp

def _softmax(x, axis=-1):
    return jax.nn.softmax(x, axis=axis)

def _gelu(x):
    return jax.nn.gelu(x, approximate=True)

def _silu(x):
    return jax.nn.silu(x)

def _sigmoid(x):
    return jax.nn.sigmoid(x)

def _layernorm(x, axis=-1, eps=1e-05):
    m = jnp.mean(x, axis=axis, keepdims=True)
    v = jnp.var(x, axis=axis, keepdims=True)
    return (x - m) / jnp.sqrt(v + eps)

def _scatter_add(tgt, idx, src, axis=0):
    return tgt.at[idx].add(src)

def _segment_sum(src, seg, n):
    return jax.ops.segment_sum(src, seg, n)
kernel_name = 'mk_gnn_preln_d1_gnn_r32_4f10e0'

def setup_inputs(seed: int=0):
    np.random.seed(seed)
    _w = jnp.asarray

    def _rec_inputs():
        import jax
        import jax.numpy as jnp
        _gk = jax.random.key(seed)
        x = -0.0003713 + 1 * jax.random.normal(jax.random.fold_in(_gk, 1), (50000, 256), jnp.float32)
        src = jax.random.randint(jax.random.fold_in(_gk, 2), (50000,), 0, 50000, jnp.int32)
        dst = jnp.minimum((50000 * jax.random.uniform(jax.random.fold_in(_gk, 3), (50000,)) ** 2.0).astype(jnp.int32), 49999)
        _o = jnp.argsort(dst, stable=True)
        src = src[_o]
        dst = dst[_o]
        edge_type_7 = jax.random.randint(jax.random.fold_in(_gk, 12), (50000,), 0, 7, jnp.int32)
        return (x, src, dst, edge_type_7)
    x, src, dst, edge_type_7 = _rec_inputs()

    def _L0_gnn_setup():
        import jax, jax.numpy as jnp
        import numpy as np
        N = 50000
        E = 350000
        IN_C = 256
        OUT_C = 256
        N_EDGE_TYPE = 7
        key = jax.random.key(seed)
        k1, k2, k3, k4 = jax.random.split(key, 4)
        x = jax.random.normal(k1, (N, IN_C), dtype=jnp.float32)
        edge_index = jax.random.randint(k2, (2, E), 0, N, dtype=jnp.int64)
        edge_type = jax.random.randint(k3, (E,), 0, N_EDGE_TYPE, dtype=jnp.int64)
        avg_degree = 7
        std = np.sqrt(2.0 / float(avg_degree * IN_C + avg_degree * OUT_C))
        a = np.sqrt(3.0) * std
        weights = jax.random.uniform(k4, (N_EDGE_TYPE * IN_C, OUT_C), dtype=jnp.float32, minval=-a, maxval=a)
        return {'x': x, 'edge_index': edge_index, 'edge_type': edge_type, 'weights': weights}
    _L0_gnn_all = _L0_gnn_setup()
    _L0_gnn_in = {k: v for k, v in _L0_gnn_all.items() if k in ('weights',)}
    del _L0_gnn_all
    return {'x': x, 'src': src, 'dst': dst, 'edge_type_7': edge_type_7, 'L0_gnn_weights': _L0_gnn_in['weights']}

def reference(x, src, dst, edge_type_7, L0_gnn_weights):
    import jax
    import jax.numpy as jnp

    def _L0_gnn_ref(x, edge_index, edge_type, weights):
        import jax, jax.numpy as jnp
        import numpy as np
        N = 50000
        E = 350000
        IN_C = 256
        OUT_C = 256
        N_EDGE_TYPE = 7
        n = x.shape[0]
        row, col = (edge_index[0], edge_index[1])
        index = row * N_EDGE_TYPE + edge_type
        num_seg = n * N_EDGE_TYPE
        gathered = x[col]
        sums = jax.ops.segment_sum(gathered, index, num_segments=num_seg)
        cnt = jax.ops.segment_sum(jnp.ones((index.shape[0],), x.dtype), index, num_segments=num_seg)
        mean = sums / jnp.maximum(cnt, 1.0)[:, None]
        return mean.reshape(n, -1) @ weights
    edge_index = jnp.stack([src, dst])
    h = jnp.maximum(_layernorm(x, axis=-1), 0.0)
    x = x + _L0_gnn_ref(h, edge_index, edge_type_7, L0_gnn_weights)
    return x

_drawn_inputs = setup_inputs


def setup_inputs(seed=0):
    import zlib

    import numpy as np

    out = dict(_drawn_inputs(seed))
    spreads = {}
    factors = {}
    for name, (base, spread) in spreads.items():
        noise = np.random.default_rng([zlib.crc32(name.encode()), seed]).standard_normal(out[name].shape)
        drawn = base * np.exp(spread * noise) if base else spread * noise
        out[name] = jnp.asarray(drawn.astype(out[name].dtype))
    for name, factor in factors.items():
        out[name] = (out[name] * factor).astype(out[name].dtype)
    return out
```

```python
from contextlib import ExitStack

import concourse.bass as bass
from concourse import mybir


ALU = mybir.AluOpType
ACT = mybir.ActivationFunctionType
AX = mybir.AxisListType
F32 = mybir.dt.float32
F16 = mybir.dt.float16
I32 = mybir.dt.int32

P = 128
EPS = 1e-5
U = 4
GROUPS = 4
WIN_P, WIN_R = 96, 2
WIN = WIN_P * WIN_R
ROW = 260
SENT = 65535
MASKED = 1024


def gnn_kernel(nc, x, src, dst, etype, weights, out):
    N, D = x.shape
    E = src.shape[0]
    T = weights.shape[0] // D
    KB = D // P
    EP = 125
    TILES = E // EP
    TG = TILES // GROUPS
    CH = (TG * EP + T * (P - 1)) // P
    NCH = GROUPS * CH
    SUP = 4 * P
    NS = -(-N // SUP)
    NB = 4 * NS
    LASTP = (N - (NS - 1) * SUP) // 4
    BODIES = TG // U
    CB = CH // U
    assert E == EP * TILES and TG % U == 0 and CH % U == 0 and 4 * CH <= 512 and NB <= 512
    assert CB == BODIES + 1 and E < SENT and N < SENT and T <= 8 and LASTP * 4 == N - (NS - 1) * SUP and NS % 2 == 0

    y_dram = nc.dram_tensor("y_by_position", (E + WIN, ROW), F32, kind="Internal").ap()

    with ExitStack() as ctx:
        def sb(name, shape, dt):
            return ctx.enter_context(nc.sbuf_tensor(name, shape, dt))

        def pb(name, shape, dt=F32):
            return ctx.enter_context(nc.psum_tensor(name, shape, dt))

        def sem(name):
            return ctx.enter_context(nc.semaphore(name))

        iota_b = sb("iota_b", [P, NB], F16)
        iota_f = sb("iota_f", [P, P], F32)
        rowidx = sb("rowidx", [P, WIN_R], F32)
        ones16 = sb("ones16", [P, P], F16)
        onesf = sb("onesf", [P, TILES], F32)
        zeros16 = sb("zeros16", [P, 512], F16)
        before16 = sb("before16", [P, P], F16)
        notbefore16 = sb("notbefore16", [P, P], F16)
        beforef = sb("beforef", [P, P], F32)
        ident16 = sb("ident16", [P, P], F16)
        identf = sb("identf", [P, P], F32)
        zrow = sb("zrow", [P, WIN_R * ROW], F32)
        W = sb("W", [P, KB, T, D], F32)
        epsc = sb("epsc", [P, 1], F32)
        src_i = sb("src_i", [P, TILES], I32)
        dst_i = sb("dst_i", [P, TILES], I32)
        typ_i = sb("typ_i", [P, TILES], I32)
        t_i = [sb(f"t_i{n}", [P, TILES], I32) for n in range(4)]
        typ_f = sb("typ_f", [P, TILES], F32)
        bucket_f = sb("bucket_f", [P, TILES], F32)
        slot_lo = sb("slot_lo", [P, TILES], F32)
        slot_hi = sb("slot_hi", [P, TILES], F32)
        pieces = sb("pieces", [P, TILES, 4], F16)
        is_type = sb("is_type", [P, T, TILES], F32)
        run_type = sb("run_type", [P, T, TILES], F32)
        tot = sb("tot", [P, 3, T * GROUPS], F32)
        tot_i = sb("tot_i", [P, 2, T * GROUPS], I32)
        nch = sb("nch", [P, GROUPS, T], F32)
        cend = sb("cend", [P, GROUPS, T], F32)
        slotbase = sb("slotbase", [P, T, GROUPS], F32)
        ctyp_w = sb("ctyp_w", [P, GROUPS, CH, T], F32)
        ctyp_f = sb("ctyp_f", [P, NCH], F32)
        ctyp_i = sb("ctyp_i", [P, NCH], I32)
        bcnt = sb("bcnt", [P, NB], F32)
        bend = sb("bend", [P, NB], F32)
        bstart = sb("bstart", [P, NB], F32)
        bstart_i = sb("bstart_i", [P, NB], I32)
        bfit = sb("bfit", [P, NB], F32)
        blen = sb("blen", [P, NB], F32)
        bend_i = sb("bend_i", [P, NB], I32)
        bcnt_i = sb("bcnt_i", [P, NB], I32)
        big = sb("big", [P, 1], F32)
        big_i = sb("big_i", [P, 1], I32)
        GW = 512
        gkey = sb("gkey", [P, GW], F32)
        bkey = sb("bkey", [P, NB], F32)
        okey = sb("okey", [P, 2], F32)
        okey_i = sb("okey_i", [P, 1], I32)
        oeq = sb("oeq", [P, GW], F32)
        ocnt = sb("ocnt", [P, 2], F32)
        minus1 = sb("minus1", [P, 1], F32)
        orow = sb("orow", [P, ROW], F32)
        oh = sb("oh", [P, U, NB], F16)
        junk = sb("junk", [P, NB], F16)
        pos4 = sb("pos4", [P, U], F32)
        pos4_i = sb("pos4_i", [P, 3, U], I32)
        ohhi = sb("ohhi", [P, U, CH], F16)
        ohlo = sb("ohlo", [P, U, P], F16)
        vals = sb("vals", [P, U, 4, CH], F16)
        m_i = sb("m_i", [P, 4, CH], I32)
        m2_i = sb("m2_i", [P, 6, CH], I32)
        dst_t = sb("dst_t", [P, NCH], I32)
        pos_t = sb("pos_t", [P, NCH], I32)
        key_t = sb("key_t", [P, NCH], F32)
        gidx = sb("gidx", [P, U], I32)
        sidx = sb("sidx", [P, U], I32)
        xg = sb("xg", [P, U, D], F32)
        st = sb("st", [P, U, 6], F32)
        mv = sb("mv", [P, U, 2], F32)
        nm = sb("nm", [P, U], F32)
        sd = sb("sd", [P, U], F32)
        rstd = sb("rstd", [P, U], F32)
        h = sb("h", [P, 2, D], F32)
        hT = sb("hT", [P, 2, D], F32)
        yb = sb("yb", [P, U, ROW], F32)
        xs = sb("xs", [P, 2, 4 * D], F32)
        ob = sb("ob", [P, 2, 4 * D], F32)
        yw = sb("yw", [P, 2, 4, WIN_R * ROW], F32)
        ge = sb("ge", [P, 2, 4, WIN_R], F32)
        keym = sb("keym", [P, 2, 4, WIN_R], F16)
        key_i = sb("key_i", [P, 2, 2, 4, WIN_R], I32)
        local = sb("local", [P, 2, 4, WIN_R], F32)
        cnt = sb("cnt", [P, 2, 4 * WIN_R], F32)
        wgt = sb("wgt", [P, 2, 4 * WIN_R], F32)
        junkc = sb("junkc", [P, 8, WIN], F16)
        sel = sb("sel", [P, 2, 8, P], F32)

        pP = pb("pP", [P, 512])
        pM = pb("pM", [P, 512])
        pT = [pb(f"pT{n}", [P, 512]) for n in range(2)]
        pY = [pb(f"pY{n}", [P, 512]) for n in range(2)]
        pK = pb("pK", [P, 2, 512])

        s_load = sem("s_load")
        s_w = sem("s_w")
        s_const = sem("s_const")
        s_zrow = sem("s_zrow")
        s_zst = sem("s_zst")
        s_init = sem("s_init")
        s_hoh = sem("s_hoh")
        s_hmm = sem("s_hmm")
        s_set = sem("s_set")
        s_rowcnt = sem("s_rowcnt")
        s_base = sem("s_base")
        s_start = sem("s_start")
        s_oh = sem("s_oh")
        s_pre = sem("s_pre")
        s_rank = sem("s_rank")
        s_run = sem("s_run")
        s_small = sem("s_small")
        s_hi = sem("s_hi")
        s_lo = sem("s_lo")
        s_val = sem("s_val")
        s_perm = sem("s_perm")
        s_mread = sem("s_mread")
        s_tab = sem("s_tab")
        s_tabs = sem("s_tabs")
        s_gidx = sem("s_gidx")
        s_sidx = sem("s_sidx")
        s_keys = sem("s_keys")
        s_gat = [sem(f"s_gat{k}") for k in range(U)]
        s_sc = [sem(f"s_sc{k}") for k in range(U)]
        s_st = sem("s_st")
        s_mv = sem("s_mv")
        s_nm = sem("s_nm")
        s_sd = sem("s_sd")
        s_rstd = sem("s_rstd")
        s_h = sem("s_h")
        s_tp = sem("s_tp")
        s_hT = sem("s_hT")
        s_y = sem("s_y")
        s_yb = sem("s_yb")
        s_win = [sem(f"s_win{n}") for n in range(2)]
        s_win_c = sem("s_win_c")
        s_key = sem("s_key")
        s_kbc = sem("s_kbc")
        s_cnt = sem("s_cnt")
        s_wgt = sem("s_wgt")
        s_sel = sem("s_sel")
        s_sum = sem("s_sum")
        s_fin = sem("s_fin")
        s_oin = sem("s_oin")
        s_ostep = sem("s_ostep")
        s_oout = sem("s_oout")
        s_out = [sem(f"s_out{n}") for n in range(2)]

        block = ctx.enter_context(nc.Block())
        CONSTS = 9
        INITS = 11
        KEYS = 4
        LOADS = 80
        TABS = 8

        @block.sync
        def _(sp):
            sp.dma_start(src_i[0:EP, :], src.rearrange("(p j) -> p j", j=TILES)).then_inc(s_load, 16)
            sp.dma_start(typ_i[0:EP, :], etype.rearrange("(p j) -> p j", j=TILES)).then_inc(s_load, 16)
            sp.dma_start(dst_i[0:EP, :], dst.rearrange("(p j) -> p j", j=TILES)).then_inc(s_load, 16)
            wv = weights.rearrange("(t b p) n -> b p t n", b=KB, p=P)
            for b in range(KB):
                sp.dma_start(W[:, b, :, :], wv[b]).then_inc(s_w, 16)
            sp.wait_ge(s_zrow, 1)
            sp.dma_start(y_dram[E:E + WIN, :].rearrange("(p r) c -> p (r c)", r=WIN_R),
                         zrow[0:WIN_P, :]).then_inc(s_zst, 16)
            sp.wait_ge(s_zst, 16)
            for k in range(U):
                sp.wait_ge(s_sc[k], 16 * NCH // U)

            def load(t, par, first, parts=P):
                s = t * 2 + par
                starts = [sp.value_load(bstart_i[0:1, bass.ds(s * 4 + w, 1)], min_val=0, max_val=E) for w in range(4)]
                if not first:
                    sp.wait_ge(s_fin, t * 8 + par * 4 - 4)
                sp.dma_start(xs[0:parts, par, :],
                             x[bass.ds(s * SUP, 4 * parts), :].rearrange("(p w) c -> p (w c)", w=4)
                             ).then_inc(s_win[par], 16)
                for w in range(4):
                    sp.dma_start(yw[0:WIN_P, par, w, :],
                                 y_dram[bass.ds(starts[w], WIN), :].rearrange("(p r) c -> p (r c)", r=WIN_R)
                                 ).then_inc(s_win[par], 16)

            load(0, 0, True)
            load(0, 1, True)
            with sp.Fori(1, NS // 2 - 1) as t:
                load(t, 0, False)
                load(t, 1, False)
            load(NS // 2 - 1, 0, False)
            load(NS // 2 - 1, 1, False, LASTP)

        def add_edge(pool, bk, e):
            steps = [0]

            def step(ins):
                steps[0] += 1
                ins.then_inc(s_ostep, 1)
                pool.wait_ge(s_ostep, steps[0])

            pool.dma_start(orow[0:1, :], y_dram[bass.ds(e, 1), :]).then_inc(s_oin, 16)
            pool.dma_start(okey[:, 0:1], y_dram[bass.ds(e, 1), D:D + 1].to_broadcast([P, 1])).then_inc(s_oin, 16)
            pool.wait_ge(s_oin, 32)
            step(pool.tensor_copy(okey_i[:, :], okey[:, 0:1]))
            key = pool.value_load(okey_i[0:1, 0:1], min_val=0, max_val=1023)
            step(pool.tensor_tensor(okey[:, 1:2], okey[:, 0:1], bkey[:, bass.ds(bk, 1)], ALU.add))
            step(pool.tensor_scalar(oeq[:, :], gkey[:, :], okey[:, 1:2], None, ALU.is_equal))
            n = GW
            while n > 1:
                n //= 2
                step(pool.tensor_tensor(oeq[:, 0:n], oeq[:, 0:n], oeq[:, n:2 * n], ALU.add))
            step(pool.partition_all_reduce(ocnt[:, 0:1], oeq[:, 0:1], P, bass.bass_isa.ReduceOp.add))
            step(pool.tensor_tensor(ocnt[:, 1:2], ocnt[:, 0:1], minus1[:, :], ALU.pow))
            step(pool.tensor_scalar(orow[0:1, 0:D], orow[0:1, 0:D], ocnt[0:1, 1:2], None, ALU.mult))
            node = nc.s_assert_within((bk // 4) * SUP + bk % 4 + (key % P) * 4, 0, N - 1)
            pool.dma_start(out[bass.ds(node, 1), :], orow[0:1, 0:D], accum_op=ALU.add).then_inc(s_oout, 16)
            pool.wait_ge(s_oout, 16)
            for s in (s_oin, s_ostep, s_oout):
                pool.sem_clear(s)
            pool.dma_reset()

        @block.gpsimd
        def _(pool):
            small = dict(allow_small_or_imprecise_dtypes=True)
            pool.iota(iota_b[:, :], [[1, NB]], base=0, channel_multiplier=0, **small).then_inc(s_const, 1)
            pool.iota(iota_f[:, :], [[1, P]], base=0, channel_multiplier=0, **small).then_inc(s_const, 1)
            pool.iota(rowidx[:, :], [[1, WIN_R]], base=0, channel_multiplier=WIN_R, **small).then_inc(s_const, 1)
            pool.wait_ge(s_init, INITS)
            for t, ones, pattern, base, mult, op in (
                    (before16, ones16, [[1, P]], 0, -1, ALU.is_gt),
                    (notbefore16, ones16, [[-1, P]], 0, 1, ALU.is_ge),
                    (beforef, onesf, [[1, P]], 0, -1, ALU.is_gt),
                    (ident16, ones16, [[1, P]], 0, -1, ALU.is_equal),
                    (identf, onesf, [[1, P]], 0, -1, ALU.is_equal)):
                pool.affine_select(out=t[:, :], in_=ones[:, 0:P], pattern=pattern, compare_op=op, fill=0.0,
                                   base=base, channel_multiplier=mult).then_inc(s_const, 1)
            pool.memset(epsc[:, :], EPS).then_inc(s_const, 1)

            last_node = pool.to_reg(N - 1)
            last_edge = pool.to_reg(E - 1)

            done = pool.alloc_register("chunk_count")
            ahead = pool.alloc_register("gathered_count")
            pool.reg_mov(done, 0)
            pool.reg_mov(ahead, U)

            def gather(k, n, used=False):
                pool.wait_ge(s_start, 1)
                pool.wait_ge(s_gidx, n)
                if used:
                    pool.wait_ge(s_h, done)
                pool.indirect_dma_start(xg[:, k, :], None, x, bass.IndirectOffsetOnAxis(ap=gidx[:, k:k + 1], axis=0),
                                        bounds_check=last_node, oob_is_err=False).then_inc(s_gat[k], 16)

            def scatter(k):
                pool.wait_ge(s_start, 1)
                pool.wait_ge(s_sidx, done)
                pool.wait_ge(s_keys, done)
                pool.wait_ge(s_yb, done)
                pool.indirect_dma_start(y_dram[:, :], bass.IndirectOffsetOnAxis(ap=sidx[:, k:k + 1], axis=0),
                                        yb[:, k, :], None, bounds_check=last_edge, oob_is_err=False
                                        ).then_inc(s_sc[k], 16)

            for k in range(U):
                gather(k, k + 1)
            with pool.Fori(0, NCH // U - 1):
                for k in range(U):
                    pool.reg_add(done, done, 1)
                    pool.reg_add(ahead, ahead, 1)
                    gather(k, ahead, True)
                    scatter(k)
            for k in range(U):
                pool.reg_add(done, done, 1)
                scatter(k)

            for n in range(2):
                pool.wait_ge(s_out[n], 16 * NS // 2)
            for k in range(U):
                pool.wait_ge(s_sc[k], 16 * NCH // U)
            most = pool.value_load(big_i[0:1, 0:1], min_val=0, max_val=E)
            with pool.If(most > WIN):
                with pool.Fori(0, NB) as bk:
                    size = pool.value_load(bcnt_i[0:1, bass.ds(bk, 1)], min_val=0, max_val=E)
                    start = pool.value_load(bstart_i[0:1, bass.ds(bk, 1)], min_val=0, max_val=E)
                    end = pool.value_load(bend_i[0:1, bass.ds(bk, 1)], min_val=0, max_val=E)
                    with pool.If(size > WIN):
                        with pool.Fori(start, end) as e:
                            add_edge(pool, bk, e)
                        pool.nop()
                    pool.nop()
                pool.nop()
            pool.nop()

        @block.vector
        def _(v):
            for t, val in ((ones16, 1.0), (onesf, 1.0), (zeros16, 0.0), (xg, 0.0), (gidx, 0), (sidx, 0),
                           (yb, 0.0)):
                v.memset(t[:], val).then_inc(s_init, 1)
            v.memset(zrow[:, :], 0.0).then_inc(s_zrow, 1)
            v.memset(gkey[:, :], -1.0).then_inc(s_init, 1)
            v.memset(minus1[:, :], -1.0).then_inc(s_init, 1)
            v.memset(junk[:, :], 0.0).then_inc(s_init, 1)
            v.memset(xs[:, :, :], 0.0).then_inc(s_init, 1)

            steps = [0]

            def link(ins):
                steps[0] += 1
                ins.then_inc(s_set, 1)
                v.wait_ge(s_set, steps[0])

            v.wait_ge(s_load, 48)
            S, Dn, Ty = src_i[0:EP, :], dst_i[0:EP, :], typ_i[0:EP, :]
            A, B, C, F = (t[0:EP, :] for t in t_i)
            link(v.tensor_scalar(A, S, 9, 2, ALU.arith_shift_right, ALU.logical_shift_left))
            link(v.tensor_scalar(B, S, 3, None, ALU.bitwise_and))
            link(v.tensor_tensor(C, A, B, ALU.bitwise_or))
            link(v.tensor_copy(bucket_f[0:EP, :], C))
            v.wait_ge(s_const, CONSTS)

            def count(i, first=False):
                for k in range(U):
                    if not first:
                        v.wait_ge(s_hmm, i * U + k - U + 1)
                    v.tensor_scalar(oh[0:EP, k, :], iota_b[0:EP, :], bucket_f[0:EP, bass.ds(i * U + k, 1)], None,
                                    ALU.is_equal).then_inc(s_hoh, 1)

            count(0, True)
            with v.Fori(1, TILES // U) as i:
                count(i)

            link(v.tensor_scalar(A, S, 2, P - 1, ALU.arith_shift_right, ALU.bitwise_and))
            link(v.tensor_scalar(B, Ty, 7, None, ALU.logical_shift_left))
            link(v.tensor_tensor(C, A, B, ALU.bitwise_or))
            link(v.tensor_copy(pieces[0:EP, :, 3], C))
            link(v.tensor_scalar(typ_f[0:EP, :], bucket_f[0:EP, :], 1024.0, None, ALU.mult))
            v.wait_ge(s_init, INITS)
            link(v.tensor_tensor(gkey[0:EP, 0:TILES], typ_f[0:EP, :], C, ALU.add))
            link(v.tensor_scalar(bkey[:, :], iota_b[:, :], 1024.0, None, ALU.mult))
            link(v.tensor_scalar(A, Dn, SENT, None, ALU.bitwise_xor))
            link(v.tensor_scalar(B, A, 2047, None, ALU.bitwise_and))
            link(v.tensor_copy(pieces[0:EP, :, 0], B))
            link(v.tensor_scalar(F, A, 11, 5, ALU.arith_shift_right, ALU.logical_shift_left))
            link(v.tensor_copy(pieces[0:EP, :, 2], F))
            link(v.tensor_copy(typ_f[0:EP, :], Ty))
            for t in range(T):
                v.tensor_scalar(is_type[0:EP, t, :], typ_f[0:EP, :], float(t), None, ALU.is_equal).then_inc(s_set, 1)
            steps[0] += T
            v.wait_ge(s_set, steps[0])
            for t in range(T):
                for g in range(GROUPS):
                    c = slice(g * TG, (g + 1) * TG)
                    v.tensor_tensor_scan(run_type[0:EP, t, c], onesf[0:EP, 0:TG], is_type[0:EP, t, c], 0.0,
                                         ALU.mult, ALU.add).then_inc(s_set, 1)
            steps[0] += T * GROUPS
            v.wait_ge(s_set, steps[0])
            v.tensor_copy(tot[0:EP, 0, :].rearrange("p (t g) -> p t g", g=GROUPS),
                          run_type[0:EP, :, :].rearrange("p t (g j) -> p t g j", g=GROUPS)[:, :, :, TG - 1]
                          ).then_inc(s_rowcnt, 1)
            v.wait_ge(s_base, 1)
            NTG = T * GROUPS
            link(v.tensor_copy(tot[:, 1:3, :].rearrange("p a b -> p (a b)"), pM[:, 0:2 * NTG]))
            link(v.tensor_scalar(tot_i[:, 0, :], tot[:, 2, :], float(P - 1), None, ALU.add))
            link(v.tensor_scalar(tot_i[:, 1, :], tot_i[:, 0, :], 7, None, ALU.arith_shift_right))
            link(v.tensor_copy(nch[:, :, :], tot_i[:, 1, :].rearrange("p (t g) -> p g t", g=GROUPS)))
            for g in range(GROUPS):
                link(v.tensor_tensor_scan(cend[:, g, :], onesf[:, 0:T], nch[:, g, :], 0.0, ALU.mult, ALU.add))
            link(v.tensor_tensor(nch[:, :, :], cend[:, :, :], nch[:, :, :], ALU.subtract))
            link(v.scalar_tensor_tensor(slotbase[0:EP, :, :], nch[0:EP, :, :].rearrange("p g t -> p t g"), float(P),
                                        tot[0:EP, 1, :].rearrange("p (t g) -> p t g", g=GROUPS), ALU.mult, ALU.add))
            for t in range(T):
                v.tensor_tensor(run_type[0:EP, t, :].rearrange("p (g j) -> p g j", g=GROUPS),
                                run_type[0:EP, t, :].rearrange("p (g j) -> p g j", g=GROUPS),
                                slotbase[0:EP, t, :].unsqueeze(2).to_broadcast([EP, GROUPS, TG]),
                                ALU.add).then_inc(s_set, 1)
            steps[0] += T
            v.wait_ge(s_set, steps[0])
            link(v.tensor_tensor(run_type[0:EP, :, :], run_type[0:EP, :, :], is_type[0:EP, :, :], ALU.mult))
            link(v.tensor_reduce(typ_f[0:EP, :], run_type[0:EP, :, :].rearrange("p t j -> p j t"), AX.X, ALU.add))
            link(v.tensor_scalar(A, typ_f[0:EP, :], -1.0, None, ALU.add))
            link(v.tensor_scalar(B, A, P - 1, None, ALU.bitwise_and))
            link(v.tensor_scalar(C, A, 7, None, ALU.arith_shift_right))
            link(v.tensor_copy(slot_lo[0:EP, :], B))
            link(v.tensor_copy(slot_hi[0:EP, :], C))
            for g in range(GROUPS):
                v.tensor_tensor(ctyp_w[:, g, :, :], iota_f[:, 0:CH].unsqueeze(2).to_broadcast([P, CH, T]),
                                cend[:, g, :].unsqueeze(1).to_broadcast([P, CH, T]), ALU.is_ge).then_inc(s_set, 1)
            steps[0] += GROUPS
            v.wait_ge(s_set, steps[0])
            link(v.tensor_reduce(ctyp_f[:, :], ctyp_w[:, :, :, :].rearrange("p g c t -> p (g c) t"), AX.X, ALU.add))
            link(v.tensor_scalar(ctyp_i[:, :], ctyp_f[:, :], float(T - 1), None, ALU.min))
            v.wait_ge(s_hmm, TILES)
            link(v.tensor_copy(bcnt[:, :], pP[:, 0:NB]))
            link(v.tensor_tensor_scan(bend[:, :], onesf[:, 0:NB], bcnt[:, :], 0.0, ALU.mult, ALU.add))
            link(v.tensor_tensor(bstart[:, :], bend[:, :], bcnt[:, :], ALU.subtract))
            link(v.tensor_copy(bstart_i[:, :], bstart[:, :]))
            link(v.tensor_scalar(bfit[:, :], bcnt[:, :], float(WIN), None, ALU.is_le))
            link(v.tensor_copy(bcnt_i[:, :], bcnt[:, :]))
            link(v.tensor_copy(bend_i[:, :], bend[:, :]))
            link(v.tensor_reduce(big[:, :], bcnt[:, :], AX.X, ALU.max))
            link(v.tensor_copy(big_i[:, :], big[:, :]))
            v.tensor_tensor(blen[:, :], bcnt[:, :], bfit[:, :], ALU.mult).then_inc(s_start, 1)
            v.wait_ge(s_start, 1)

            def rank_hot(m, k, first):
                if not first:
                    v.wait_ge(s_run, m * U + k - U + 1)
                v.tensor_scalar(oh[0:EP, k, :], iota_b[0:EP, :], bucket_f[0:EP, bass.ds(m * U + k, 1)], None,
                                ALU.is_equal).then_inc(s_oh, 1)

            def rank_read(m, k, first):
                v.wait_ge(s_pre, m * U + k + 1)
                if not first and k == 0:
                    v.wait_ge(s_small, m * 5)
                v.tensor_tensor_reduce(junk[0:EP, :], oh[0:EP, k, :], pP[0:EP, 0:NB], 1.0, 0.0, ALU.mult, ALU.add,
                                       pos4[0:EP, k:k + 1]).then_inc(s_rank, 1)

            def rank_split(m):
                v.wait_ge(s_rank, m * U + U)
                v.tensor_scalar(pos4_i[0:EP, 0, :], pos4[0:EP, :], -1.0, float(SENT), ALU.mult, ALU.add
                                ).then_inc(s_small, 1)
                v.wait_ge(s_small, m * 5 + 1)
                v.tensor_scalar(pos4_i[0:EP, 1, :], pos4_i[0:EP, 0, :], 2047, None, ALU.bitwise_and
                                ).then_inc(s_small, 1)
                v.tensor_scalar(pos4_i[0:EP, 2, :], pos4_i[0:EP, 0, :], 11, None, ALU.arith_shift_right
                                ).then_inc(s_small, 1)
                v.wait_ge(s_small, m * 5 + 3)
                v.tensor_copy(pieces[0:EP, bass.ds(m * U, U), 1], pos4_i[0:EP, 1, :]).then_inc(s_small, 1)
                v.tensor_tensor(pieces[0:EP, bass.ds(m * U, U), 2], pieces[0:EP, bass.ds(m * U, U), 2],
                                pos4_i[0:EP, 2, :], ALU.add).then_inc(s_small, 1)

            def perm_hot(m, k, first):
                if not first:
                    v.wait_ge(s_perm, m * U + k - U + 1)
                v.tensor_scalar(ohhi[0:EP, k, :], iota_b[0:EP, 0:CH], slot_hi[0:EP, bass.ds(m * U + k, 1)], None,
                                ALU.is_equal).then_inc(s_hi, 1)
                v.tensor_scalar(ohlo[0:EP, k, :], iota_b[0:EP, 0:P], slot_lo[0:EP, bass.ds(m * U + k, 1)], None,
                                ALU.is_equal).then_inc(s_lo, 1)

            def perm_vals(m, k):
                v.wait_ge(s_hi, m * U + k + 1)
                if k == 0:
                    v.wait_ge(s_small, m * 5 + 5)
                v.tensor_tensor(vals[0:EP, k, :, :], ohhi[0:EP, k, :].unsqueeze(1).to_broadcast([EP, 4, CH]),
                                pieces[0:EP, bass.ds(m * U + k, 1), :].rearrange("p a b -> p (a b)")
                                .unsqueeze(2).to_broadcast([EP, 4, CH]), ALU.mult).then_inc(s_val, 1)

            def prep(m, rank, perm, first_rank=False, first_perm=False):
                if rank:
                    for k in range(U):
                        rank_hot(m, k, first_rank)
                for k in range(U):
                    if perm:
                        perm_hot(m - 1, k, first_perm)
                    if rank:
                        rank_read(m, k, first_rank)
                    if perm:
                        perm_vals(m - 1, k)
                if rank:
                    rank_split(m)

            def tables(g):
                v.wait_ge(s_perm, (g + 1) * TG)
                v.tensor_copy(m_i[:, :, :].rearrange("p a c -> p (a c)"), pM[:, 0:4 * CH]).then_inc(s_tab, 1)
                n = g * TABS
                c = bass.ds(g * CH, CH)
                v.wait_ge(s_tab, n + 1)
                v.tensor_copy(key_t[:, c], m_i[:, 3, :]).then_inc(s_tab, 1)
                v.tensor_scalar(m2_i[:, 0, :], m_i[:, 2, :], 5, 11, ALU.arith_shift_right, ALU.logical_shift_left
                                ).then_inc(s_tab, 1)
                v.tensor_scalar(m2_i[:, 1, :], m_i[:, 2, :], 31, 11, ALU.bitwise_and, ALU.logical_shift_left
                                ).then_inc(s_tab, 1)
                v.wait_ge(s_tab, n + 4)
                v.tensor_tensor(m2_i[:, 2, :], m2_i[:, 0, :], m_i[:, 0, :], ALU.bitwise_or).then_inc(s_tab, 1)
                v.tensor_tensor(m2_i[:, 3, :], m2_i[:, 1, :], m_i[:, 1, :], ALU.bitwise_or).then_inc(s_tab, 1)
                v.wait_ge(s_tab, n + 6)
                v.tensor_scalar(dst_t[:, c], m2_i[:, 2, :], SENT, None, ALU.bitwise_xor).then_inc(s_tab, 1)
                v.tensor_scalar(pos_t[:, c], m2_i[:, 3, :], SENT, None, ALU.bitwise_xor).then_inc(s_tab, 1)

            prep(0, True, False, True)
            prep(1, True, True, False, True)
            with v.Fori(2, BODIES) as m:
                prep(m, True, True)
            prep(BODIES, False, True)
            tables(0)
            with v.Fori(1, GROUPS) as g:
                prep(g * BODIES, True, False)
                with v.Fori(1, BODIES) as i:
                    prep(g * BODIES + i, True, True)
                prep(g * BODIES + BODIES, False, True)
                tables(g)

            v.wait_ge(s_tab, GROUPS * TABS)

            def gather_index(c, k):
                v.tensor_copy(gidx[:, k:k + 1], dst_t[:, bass.ds(c, 1)]).then_inc(s_gidx, 1)

            def scatter_index(b, c, k, first):
                if not first:
                    v.wait_ge(s_sc[k], b * 16)
                v.tensor_copy(sidx[:, k:k + 1], pos_t[:, bass.ds(c, 1)]).then_inc(s_sidx, 1)
                v.tensor_copy(yb[:, k, D:D + 1], key_t[:, bass.ds(c, 1)]).then_inc(s_keys, 1)

            def inverse(c, k):
                v.wait_ge(s_sd, c + 1)
                v.reciprocal(rstd[:, k:k + 1], sd[:, k:k + 1]).then_inc(s_rstd, 1)

            def chunk_turn(b, first=False, last=False):
                for k in range(U):
                    c = b * U + k
                    scatter_index(b, c, k, first)
                    v.wait_ge(s_gat[k], b * 16 + 16)
                    if not last:
                        gather_index(c + U, k)
                    v.bn_stats(st[:, k, :], xg[:, k, :]).then_inc(s_st, 1)
                    v.wait_ge(s_st, c + 1)
                    if not (first and k == 0):
                        inverse(c - 1, (k - 1) % U)
                    v.bn_aggr(mv[:, k, :], st[:, k, :]).then_inc(s_mv, 1)
                    v.wait_ge(s_mv, c + 1)
                    v.tensor_scalar(nm[:, k:k + 1], mv[:, k, 0:1], -1.0, None, ALU.mult).then_inc(s_nm, 1)

            for k in range(U):
                gather_index(k, k)
            chunk_turn(0, True)
            with v.Fori(1, NCH // U - 1) as b:
                chunk_turn(b)
            chunk_turn(NCH // U - 1, False, True)
            inverse(NCH - 1, U - 1)

            def window_turn(s, par, turn=None):
                q = slice(0, WIN_P)
                v.wait_ge(s_win[par], (0 if turn is None else turn * LOADS) + LOADS)
                key = yw[q, par, :, :].rearrange("p w (r c) -> p w r c", r=WIN_R)[:, :, :, D]
                b4 = blen[q, bass.ds(s * 4, 4)].unsqueeze(2).to_broadcast([WIN_P, 4, WIN_R])
                r4 = rowidx[q, :].unsqueeze(1).to_broadcast([WIN_P, 4, WIN_R])
                v.tensor_tensor(ge[q, par, :, :], r4, b4, ALU.is_ge).then_inc(s_key, 1)
                v.tensor_copy(key_i[q, par, 0, :, :], key).then_inc(s_key, 1)
                v.wait_ge(s_key, s * KEYS + 2)
                v.scalar_tensor_tensor(keym[q, par, :, :], ge[q, par, :, :], float(MASKED), key, ALU.mult, ALU.max
                                       ).then_inc(s_key, 1)
                v.tensor_scalar(key_i[q, par, 1, :, :], key_i[q, par, 0, :, :], P - 1, None, ALU.bitwise_and
                                ).then_inc(s_key, 1)
                v.wait_ge(s_key, s * KEYS + 4)
                v.scalar_tensor_tensor(local[q, par, :, :], ge[q, par, :, :], float(P), key_i[q, par, 1, :, :],
                                       ALU.mult, ALU.add).then_inc(s_wgt, 1)
                v.wait_ge(s_kbc, s + 1)
                for w in range(4):
                    for r in range(WIN_R):
                        a = w * WIN_R + r
                        v.tensor_scalar(junkc[q, a, :], pK[q, w // 2, (w % 2) * WIN:(w % 2) * WIN + WIN],
                                        keym[q, par, w, r:r + 1], 0.0, ALU.is_equal, ALU.add,
                                        accum_out=cnt[q, par, a:a + 1]).then_inc(s_cnt, 1)
                v.wait_ge(s_cnt, s * 8 + 8)
                v.reciprocal(wgt[q, par, :], cnt[q, par, :]).then_inc(s_wgt, 1)
                v.wait_ge(s_wgt, s * 2 + 2)
                for w in range(4):
                    for r in range(WIN_R):
                        a = w * WIN_R + r
                        v.tensor_scalar(sel[q, par, a, :], iota_f[q, :], local[q, par, w, r:r + 1],
                                        wgt[q, par, a:a + 1], ALU.is_equal, ALU.mult).then_inc(s_sel, 1)
                if turn is not None:
                    v.wait_ge(s_out[par], turn * 16)

            def finish_turn(s, par, parts=P):
                for w in range(4):
                    v.wait_ge(s_sum, s * 4 + w + 1)
                    v.tensor_tensor(ob[0:parts, par, w * D:(w + 1) * D], pY[w % 2][0:parts, 0:D],
                                    xs[0:parts, par, w * D:(w + 1) * D], ALU.add).then_inc(s_fin, 1)

            window_turn(0, 0)
            window_turn(1, 1)
            finish_turn(0, 0)
            with v.Fori(1, NS // 2) as t:
                window_turn(t * 2, 0, t)
                finish_turn(t * 2 - 1, 1)
                window_turn(t * 2 + 1, 1, t)
                finish_turn(t * 2, 0)
            finish_turn(NS - 1, 1, LASTP)

        @block.tensor
        def _(pe):
            def mm(o, a, b, **k):
                return pe.matmul(o, a, b, skip_group_check=True, **k)

            pe.wait_ge(s_const, CONSTS)
            pe.wait_ge(s_init, INITS)

            def count(i, first=False):
                for k in range(U):
                    pe.wait_ge(s_hoh, i * U + k + 1)
                    mm(pP[:, 0:NB], ones16[0:EP, :], oh[0:EP, k, :], start=first and k == 0, stop=True
                       ).then_inc(s_hmm, 1)

            count(0, True)
            with pe.Fori(1, TILES // U) as i:
                count(i)

            NTG = T * GROUPS
            pe.wait_ge(s_rowcnt, 1)
            mm(pM[:, 0:NTG], beforef[0:EP, :], tot[0:EP, 0, :], start=True, stop=True)
            mm(pM[:, NTG:2 * NTG], onesf[0:EP, 0:P], tot[0:EP, 0, :], start=True, stop=True).then_inc(s_base, 1)
            pe.wait_ge(s_start, 1)
            mm(pP[0:EP, 0:NB], onesf[0:1, 0:EP], bstart[0:1, :], start=True, stop=True)

            def rank_in_tile(n, k):
                pe.wait_ge(s_oh, n + 1)
                mm(pP[0:EP, 0:NB], before16[0:EP, 0:EP], oh[0:EP, k, :], start=False, stop=True).then_inc(s_pre, 1)

            def rank_rest(n, k):
                pe.wait_ge(s_rank, n + 1)
                mm(pP[0:EP, 0:NB], notbefore16[0:EP, 0:EP], oh[0:EP, k, :], start=False, stop=True
                   ).then_inc(s_run, 1)

            def permute(n, k):
                pe.wait_ge(s_lo, n + 1)
                pe.wait_ge(s_val, n + 1)
                mm(pM[:, 0:4 * CH], ohlo[0:EP, k, :], vals[0:EP, k, :, :].rearrange("p a c -> p (a c)"),
                   start=False, stop=True).then_inc(s_perm, 1)

            def prep(m, rank, perm):
                if rank:
                    rank_in_tile(m * U, 0)
                for k in range(U):
                    if rank:
                        rank_rest(m * U + k, k)
                        if k + 1 < U:
                            rank_in_tile(m * U + k + 1, k + 1)
                    if perm:
                        permute((m - 1) * U + k, k)

            def clear_slots():
                mm(pM[:, 0:4 * CH], zeros16[0:EP, 0:P], zeros16[0:EP, 0:4 * CH], start=True, stop=True)

            prep(0, True, False)
            clear_slots()
            with pe.Fori(1, BODIES) as m:
                prep(m, True, True)
            prep(BODIES, False, True)
            with pe.Fori(1, GROUPS) as g:
                prep(g * BODIES, True, False)
                pe.wait_ge(s_tab, g * TABS - TABS + 1)
                clear_slots()
                with pe.Fori(1, BODIES) as i:
                    prep(g * BODIES + i, True, True)
                prep(g * BODIES + BODIES, False, True)

            pe.wait_ge(s_w, 16 * KB)

            def chunk(c, k, typ, first):
                pe.wait_ge(s_h, c + 1)
                for b in range(KB):
                    t = pe.transpose(pT[k % 2][:, b * P:(b + 1) * P], h[:, k % 2, b * P:(b + 1) * P], identf[:, :])
                t.then_inc(s_tp, 1)
                pe.wait_ge(s_hT, c + 1)
                if not (first and k < 2):
                    pe.wait_ge(s_yb, c - 1)
                for b in range(KB):
                    t = mm(pY[k % 2][:, 0:D], hT[:, k % 2, b * P:(b + 1) * P],
                           W[:, b, bass.ds(typ, 1), :].rearrange("p a d -> p (a d)"), start=b == 0, stop=b == KB - 1)
                t.then_inc(s_y, 1)

            def chunk_turn(b, first=False):
                types = [pe.value_load(ctyp_i[0:1, bass.ds(b * U + k, 1)], min_val=0, max_val=T - 1)
                         for k in range(U)]
                for k in range(U):
                    chunk(b * U + k, k, types[k], first)

            chunk_turn(0, True)
            with pe.Fori(1, NCH // U) as b:
                chunk_turn(b)

            def key_rows(s, par, first=False):
                pe.wait_ge(s_key, s * KEYS + 3)
                if not first:
                    pe.wait_ge(s_cnt, s * 8)
                for w in range(4):
                    for r in range(WIN_R):
                        o = (w % 2) * WIN + r * WIN_P
                        t = mm(pK[:, w // 2, o:o + WIN_P], keym[0:WIN_P, par, w, r:r + 1].to_broadcast([WIN_P, P]),
                               ident16[0:WIN_P, 0:WIN_P], start=True, stop=True)
                t.then_inc(s_kbc, 1)

            def sums(s, par, first=False):
                for w in range(4):
                    pe.wait_ge(s_sel, s * 8 + w * 2 + 2)
                    if not (first and w < 2):
                        pe.wait_ge(s_fin, s * 4 + w - 1)
                    for r in range(WIN_R):
                        t = mm(pY[w % 2][:, 0:D], sel[0:WIN_P, par, w * WIN_R + r, :],
                               yw[0:WIN_P, par, w, r * ROW:r * ROW + D], start=r == 0, stop=r == WIN_R - 1)
                    t.then_inc(s_sum, 1)

            key_rows(0, 0, True)
            key_rows(1, 1)
            sums(0, 0, True)
            with pe.Fori(1, NS // 2) as t:
                key_rows(t * 2, 0)
                sums(t * 2 - 1, 1)
                key_rows(t * 2 + 1, 1)
                sums(t * 2, 0)
            sums(NS - 1, 1)

        @block.scalar
        def _(act):
            act.wait_ge(s_const, CONSTS)

            def centre(c, k):
                act.wait_ge(s_nm, c + 1)
                act.activation(h[:, k % 2, :], xg[:, k, :], ACT.Relu, bias=nm[:, k:k + 1]).then_inc(s_h, 1)
                act.activation(sd[:, k:k + 1], mv[:, k, 1:2], ACT.Sqrt, bias=epsc[:, :]).then_inc(s_sd, 1)

            def evacuate(c, k):
                act.wait_ge(s_y, c + 1)
                act.wait_ge(s_rstd, c + 1)
                act.wait_ge(s_sidx, c + 1)
                act.activation(yb[:, k, 0:D], pY[k % 2][:, 0:D], ACT.Copy, scale=rstd[:, k:k + 1]).then_inc(s_yb, 1)

            def transposed(c, k):
                act.wait_ge(s_tp, c + 1)
                act.activation(hT[:, k % 2, :], pT[k % 2][:, 0:D], ACT.Copy).then_inc(s_hT, 1)

            def chunk_turn(b, first=False):
                for k in range(U):
                    centre(b * U + k, k)
                    if not (first and k == 0):
                        evacuate(b * U + k - 1, (k - 1) % U)
                    transposed(b * U + k, k)

            chunk_turn(0, True)
            with act.Fori(1, NCH // U) as b:
                chunk_turn(b)
            evacuate(NCH - 1, U - 1)

            def store(s, par, parts=P):
                act.wait_ge(s_fin, s * 4 + 4)
                act.dma_start(out[bass.ds(s * SUP, 4 * parts), :].rearrange("(p w) c -> p (w c)", w=4),
                              ob[0:parts, par, :]).then_inc(s_out[par], 16)

            with act.Fori(0, NS // 2 - 1) as t:
                store(t * 2, 0)
                store(t * 2 + 1, 1)
            store(NS - 2, 0)
            store(NS - 1, 1, LASTP)
            for n in range(2):
                act.wait_ge(s_out[n], 16 * NS // 2)


_INS = ["x", "src", "dst", "edge_type_7", "L0_gnn_weights"]


def kernel(**inputs):
    import numpy as _np
    import concourse.bacc as _bacc
    from concourse import mybir as _mybir
    from concourse.bass_utils import run_bass_kernel_spmd as _run

    nc = _bacc.Bacc("TRN2", target_bir_lowering=False, num_devices=1)
    arrays, args = {}, []
    for name in _INS:
        a = _np.ascontiguousarray(inputs[name])
        arrays[f"in_{name}_dram"] = a
        args.append(nc.dram_tensor(f"in_{name}_dram", a.shape, _mybir.dt.from_np(a.dtype), kind="ExternalInput").ap())
    shape = inputs["x"].shape
    args.append(nc.dram_tensor("out_0_dram", shape, _mybir.dt.float32, kind="ExternalOutput").ap())
    gnn_kernel(nc, *args)
    r = _run(nc, [arrays], core_ids=[0])
    return r.results[0]["out_0_dram"]
```

```python
from contextlib import ExitStack

import concourse.bass as bass
from concourse import mybir


ALU = mybir.AluOpType
ACT = mybir.ActivationFunctionType
AX = mybir.AxisListType
F32 = mybir.dt.float32
F16 = mybir.dt.float16
I32 = mybir.dt.int32

P = 128
EPS = 1e-5
U = 4
R = 2 * U
AHEAD = 3
RS = 4
GROUPS = 4
WIN_P, WIN_R = 96, 2
WIN = WIN_P * WIN_R
ROW = 260
SENT = 65535
MASKED = 1024


def gnn_kernel(nc, x, src, dst, etype, weights, out):
    N, D = x.shape
    E = src.shape[0]
    T = weights.shape[0] // D
    KB = D // P
    EP = 125
    TILES = E // EP
    TG = TILES // GROUPS
    CH = (TG * EP + T * (P - 1)) // P
    NCH = GROUPS * CH
    SUP = 4 * P
    NS = -(-N // SUP)
    NB = 4 * NS
    LASTP = (N - (NS - 1) * SUP) // 4
    RB = TG // U
    CB = CH // U
    assert E == EP * TILES and TG % U == 0 and CH % U == 0 and 4 * CH <= 512 and NB <= 512
    assert CB == RB + 1 and CH % R == 0 and (CB - AHEAD - 1) % 2 == 0 and NS % RS == 2 and E < SENT and N < SENT and T <= 8 and LASTP * 4 == N - (NS - 1) * SUP

    y_dram = nc.dram_tensor("y_by_position", (E + WIN, ROW), F32, kind="Internal").ap()

    with ExitStack() as ctx:
        def sb(name, shape, dt):
            return ctx.enter_context(nc.sbuf_tensor(name, shape, dt))

        def pb(name, shape, dt=F32):
            return ctx.enter_context(nc.psum_tensor(name, shape, dt))

        def sem(name):
            return ctx.enter_context(nc.semaphore(name))

        iota_b = sb("iota_b", [P, NB], F16)
        iota_f = sb("iota_f", [P, P], F32)
        rowidx = sb("rowidx", [P, WIN_R], F32)
        ones16 = sb("ones16", [P, P], F16)
        onesf = sb("onesf", [P, TILES], F32)
        zeros16 = sb("zeros16", [P, 512], F16)
        before16 = sb("before16", [P, P], F16)
        notbefore16 = sb("notbefore16", [P, P], F16)
        beforef = sb("beforef", [P, P], F32)
        ident16 = sb("ident16", [P, P], F16)
        identf = sb("identf", [P, P], F32)
        zrow = sb("zrow", [P, WIN_R * ROW], F32)
        W = sb("W", [P, KB, T, D], F32)
        epsc = sb("epsc", [P, 1], F32)
        src_i = sb("src_i", [P, TILES], I32)
        dst_i = sb("dst_i", [P, TILES], I32)
        typ_i = sb("typ_i", [P, TILES], I32)
        t_i = [sb(f"t_i{n}", [P, TILES], I32) for n in range(4)]
        typ_f = sb("typ_f", [P, TILES], F32)
        bucket_f = sb("bucket_f", [P, TILES + 1], F32)
        slot_lo = sb("slot_lo", [P, TILES], F32)
        slot_hi = sb("slot_hi", [P, TILES], F32)
        lows = sb("lows", [P, TILES, 2], F16)
        highs = sb("highs", [P, TILES], F32)
        keys = sb("keys", [P, TILES], F32)
        YW = RS * 4 * WIN_R * ROW
        space = sb("space", [P, max(YW, 2 * T * TILES + NCH * T)], F32)
        is_type = space[:, 0:T * TILES].rearrange("p (t j) -> p t j", t=T)
        run_type = space[:, T * TILES:2 * T * TILES].rearrange("p (t j) -> p t j", t=T)
        ctyp_w = space[:, 2 * T * TILES:2 * T * TILES + NCH * T].rearrange("p (g c t) -> p g c t", g=GROUPS, c=CH)
        yw = space[:, 0:YW].rearrange("p (n w c) -> p n w c", n=RS, w=4)
        tot = sb("tot", [P, 3, T * GROUPS], F32)
        tot_i = sb("tot_i", [P, 2, T * GROUPS], I32)
        nch = sb("nch", [P, GROUPS, T], F32)
        cend = sb("cend", [P, GROUPS, T], F32)
        slotbase = sb("slotbase", [P, T, GROUPS], F32)
        ctyp_f = sb("ctyp_f", [P, NCH], F32)
        ctyp_i = sb("ctyp_i", [P, NCH], I32)
        bcnt = sb("bcnt", [P, NB], F32)
        bend = sb("bend", [P, NB], F32)
        bstart = sb("bstart", [P, NB], F32)
        bstart_i = sb("bstart_i", [P, NB], I32)
        bfit = sb("bfit", [P, NB], F32)
        blen = sb("blen", [P, NB], F32)
        bend_i = sb("bend_i", [P, NB], I32)
        bcnt_i = sb("bcnt_i", [P, NB], I32)
        big = sb("big", [P, 1], F32)
        big_i = sb("big_i", [P, 1], I32)
        GW = 512
        gkey = sb("gkey", [P, GW], F32)
        bkey = sb("bkey", [P, NB], F32)
        okey = sb("okey", [P, 2], F32)
        okey_i = sb("okey_i", [P, 1], I32)
        oeq = sb("oeq", [P, GW], F32)
        ocnt = sb("ocnt", [P, 2], F32)
        minus1 = sb("minus1", [P, 1], F32)
        orow = sb("orow", [P, ROW], F32)
        super_f = sb("super_f", [P, TILES], F32)
        sub_f = sb("sub_f", [P, TILES], F32)
        is_sub = sb("is_sub", [P, TILES, 4], F16)
        hist = sb("hist", [P, 4], F32)
        oh = sb("oh", [P, U, NB], F16)
        junk = sb("junk", [P, NB], F16)
        pos4 = sb("pos4", [P, U], F32)
        pos4_i = sb("pos4_i", [P, 3, U], I32)
        ohhi = sb("ohhi", [P, U, CH], F16)
        ohlo = sb("ohlo", [P, U, P], F16)
        vals = sb("vals", [P, U, 4, CH], F16)
        m_i = sb("m_i", [P, 4, CH], I32)
        m2_i = sb("m2_i", [P, 6, CH], I32)
        dst_t = sb("dst_t", [P, NCH], I32)
        pos_t = sb("pos_t", [P, NCH], I32)
        key_t = sb("key_t", [P, NCH], F32)
        gidx = sb("gidx", [P, R], I32)
        sidx = sb("sidx", [P, R], I32)
        xg = sb("xg", [P, R, D], F32)
        st = sb("st", [P, R, 6], F32)
        mv = sb("mv", [P, R, 2], F32)
        nm = sb("nm", [P, R], F32)
        sd = sb("sd", [P, R], F32)
        rstd = sb("rstd", [P, R], F32)
        h = sb("h", [P, 4, D], F32)
        hT = sb("hT", [P, 4, D], F32)
        yb = sb("yb", [P, R, ROW], F32)
        xs = sb("xs", [P, RS, 4 * D], F32)
        ob = sb("ob", [P, 2, 4 * D], F32)
        ge = sb("ge", [P, 2, 4, WIN_R], F32)
        keym = sb("keym", [P, 2, 4, WIN_R], F16)
        key_i = sb("key_i", [P, 2, 2, 4, WIN_R], I32)
        local = sb("local", [P, 2, 4, WIN_R], F32)
        krow = sb("krow", [P, 2, 4 * WIN], F16)
        cnt = sb("cnt", [P, 2, 4 * WIN_R], F32)
        wgt = sb("wgt", [P, 2, 4 * WIN_R], F32)
        junkc = sb("junkc", [P, 8, WIN], F16)
        sel = sb("sel", [P, 2, 8, P], F32)

        pP = pb("pP", [P, 512])
        pM = pb("pM", [P, 512])
        pT = [pb(f"pT{n}", [P, 512]) for n in range(2)]
        pY = [pb(f"pY{n}", [P, 512]) for n in range(2)]
        pK = pb("pK", [P, 2, 512])
        pS = [*pY, *pT]

        s_load = sem("s_load")
        s_w = sem("s_w")
        s_const = sem("s_const")
        s_zrow = sem("s_zrow")
        s_zst = sem("s_zst")
        s_init = sem("s_init")
        s_hoh = sem("s_hoh")
        s_hmm = sem("s_hmm")
        s_set = sem("s_set")
        s_hrow = sem("s_hrow")
        s_rowcnt = sem("s_rowcnt")
        s_base = sem("s_base")
        s_start = sem("s_start")
        s_oh = sem("s_oh")
        s_pre = sem("s_pre")
        s_rank = sem("s_rank")
        s_run = sem("s_run")
        s_small = sem("s_small")
        s_hi = sem("s_hi")
        s_lo = sem("s_lo")
        s_val = sem("s_val")
        s_vala = sem("s_vala")
        s_perm = sem("s_perm")
        s_mread = sem("s_mread")
        s_tab = sem("s_tab")
        s_tabs = sem("s_tabs")
        s_gidx = sem("s_gidx")
        s_sidx = sem("s_sidx")
        s_keys = sem("s_keys")
        s_gat = [sem(f"s_gat{k}") for k in range(R)]
        s_sc = [sem(f"s_sc{k}") for k in range(R)]
        s_st = sem("s_st")
        s_mv = sem("s_mv")
        s_nm = sem("s_nm")
        s_sd = sem("s_sd")
        s_rstd = sem("s_rstd")
        s_h = sem("s_h")
        s_tp = sem("s_tp")
        s_hT = sem("s_hT")
        s_y = sem("s_y")
        s_yb = sem("s_yb")
        s_win = [sem(f"s_win{n}") for n in range(RS)]
        s_key = sem("s_key")
        s_kbc = sem("s_kbc")
        s_krow = sem("s_krow")
        s_krowh = sem("s_krowh")
        s_cnt = sem("s_cnt")
        s_wgt = sem("s_wgt")
        s_inv = sem("s_inv")
        s_sel = sem("s_sel")
        s_sum = sem("s_sum")
        s_fin = sem("s_fin")
        s_oin = sem("s_oin")
        s_ostep = sem("s_ostep")
        s_oout = sem("s_oout")
        s_out = [sem(f"s_out{n}") for n in range(2)]

        block = ctx.enter_context(nc.Block())
        CONSTS = 9
        INITS = 10
        KEYS = 4
        LOADS = 80
        TABS = 8

        def schedule(eng, turn):
            NONE = (0, False, False, None, None)
            LONE = (CB - AHEAD - 1) // 2

            def plain(m):
                return [(m, True, True, None, None), (m + 1, True, True, None, None)]

            def seam(g, more):
                q = g * CB + 2 * LONE
                m = g * RB + 2 * RB
                first = (m, False, True, g + 1, None)
                turn(q, [first, (m, True, False, None, g + 1) if more else NONE])
                turn(q + 2, plain(m + 1) if more else [NONE, NONE], tabs=g + 1)

            turn(0, plain(RB + AHEAD), first=True)
            with eng.Fori(1, LONE) as i:
                turn(i * 2, plain(i * 2 + RB + AHEAD))
            with eng.Fori(0, GROUPS - 2) as g:
                seam(g, True)
                with eng.Fori(0, LONE) as i:
                    turn(g * CB + CB + i * 2, plain(g * RB + 2 * RB + AHEAD + i * 2))
            seam(GROUPS - 2, False)
            with eng.Fori(0, CB // 2 - 1) as i:
                turn(i * 2 + (GROUPS - 1) * CB, [NONE, NONE])
            turn(GROUPS * CB - 2, [NONE, NONE], last=True)

        @block.sync
        def _(sp):
            sp.dma_start(src_i[0:EP, :], src.rearrange("(p j) -> p j", j=TILES)).then_inc(s_load, 16)
            sp.dma_start(typ_i[0:EP, :], etype.rearrange("(p j) -> p j", j=TILES)).then_inc(s_load, 16)
            sp.dma_start(dst_i[0:EP, :], dst.rearrange("(p j) -> p j", j=TILES)).then_inc(s_load, 16)
            wv = weights.rearrange("(t b p) n -> b p t n", b=KB, p=P)
            for b in range(KB):
                sp.dma_start(W[:, b, :, :], wv[b]).then_inc(s_w, 16)
            sp.wait_ge(s_zrow, 1)
            sp.dma_start(y_dram[E:E + WIN, :].rearrange("(p r) c -> p (r c)", r=WIN_R),
                         zrow[0:WIN_P, :]).then_inc(s_zst, 16)
            sp.wait_ge(s_zst, 16)
            for k in range(R):
                sp.wait_ge(s_sc[k], 16 * NCH // R)

            def load(s, j, first, parts=P):
                starts = [sp.value_load(bstart_i[0:1, bass.ds(s * 4 + w, 1)], min_val=0, max_val=E) for w in range(4)]
                if not first:
                    sp.wait_ge(s_fin, s * 4 - 4 * RS + 4)
                sp.dma_start(xs[0:parts, j, :],
                             x[bass.ds(s * SUP, 4 * parts), :].rearrange("(p w) c -> p (w c)", w=4)
                             ).then_inc(s_win[j], 16)
                for w in range(4):
                    sp.dma_start(yw[0:WIN_P, j, w, :],
                                 y_dram[bass.ds(starts[w], WIN), :].rearrange("(p r) c -> p (r c)", r=WIN_R)
                                 ).then_inc(s_win[j], 16)

            for j in range(RS):
                load(j, j, True)
            with sp.Fori(1, NS // RS) as t:
                for j in range(RS):
                    load(t * RS + j, j, False)
            load(NS - 2, 0, False)
            load(NS - 1, 1, False, LASTP)

        def add_edge(pool, bk, e):
            steps = [0]

            def step(ins):
                steps[0] += 1
                ins.then_inc(s_ostep, 1)
                pool.wait_ge(s_ostep, steps[0])

            pool.dma_start(orow[0:1, :], y_dram[bass.ds(e, 1), :]).then_inc(s_oin, 16)
            pool.dma_start(okey[:, 0:1], y_dram[bass.ds(e, 1), D:D + 1].to_broadcast([P, 1])).then_inc(s_oin, 16)
            pool.wait_ge(s_oin, 32)
            step(pool.tensor_copy(okey_i[:, :], okey[:, 0:1]))
            key = pool.value_load(okey_i[0:1, 0:1], min_val=0, max_val=1023)
            step(pool.tensor_tensor(okey[:, 1:2], okey[:, 0:1], bkey[:, bass.ds(bk, 1)], ALU.add))
            step(pool.tensor_scalar(oeq[:, :], gkey[:, :], okey[:, 1:2], None, ALU.is_equal))
            n = GW
            while n > 1:
                n //= 2
                step(pool.tensor_tensor(oeq[:, 0:n], oeq[:, 0:n], oeq[:, n:2 * n], ALU.add))
            step(pool.partition_all_reduce(ocnt[:, 0:1], oeq[:, 0:1], P, bass.bass_isa.ReduceOp.add))
            step(pool.tensor_tensor(ocnt[:, 1:2], ocnt[:, 0:1], minus1[:, :], ALU.pow))
            step(pool.tensor_scalar(orow[0:1, 0:D], orow[0:1, 0:D], ocnt[0:1, 1:2], None, ALU.mult))
            node = nc.s_assert_within((bk // 4) * SUP + bk % 4 + (key % P) * 4, 0, N - 1)
            pool.dma_start(out[bass.ds(node, 1), :], orow[0:1, 0:D], accum_op=ALU.add).then_inc(s_oout, 16)
            pool.wait_ge(s_oout, 16)
            for s in (s_oin, s_ostep, s_oout):
                pool.sem_clear(s)
            pool.dma_reset()

        @block.gpsimd
        def _(pool):
            small = dict(allow_small_or_imprecise_dtypes=True)
            pool.iota(iota_b[:, :], [[1, NB]], base=0, channel_multiplier=0, **small).then_inc(s_const, 1)
            pool.iota(iota_f[:, :], [[1, P]], base=0, channel_multiplier=0, **small).then_inc(s_const, 1)
            pool.iota(rowidx[:, :], [[1, WIN_R]], base=0, channel_multiplier=WIN_R, **small).then_inc(s_const, 1)
            pool.wait_ge(s_init, INITS)
            for t, ones, pattern, base, mult, op in (
                    (before16, ones16, [[1, P]], 0, -1, ALU.is_gt),
                    (notbefore16, ones16, [[-1, P]], 0, 1, ALU.is_ge),
                    (beforef, onesf, [[1, P]], 0, -1, ALU.is_gt),
                    (ident16, ones16, [[1, P]], 0, -1, ALU.is_equal),
                    (identf, onesf, [[1, P]], 0, -1, ALU.is_equal)):
                pool.affine_select(out=t[:, :], in_=ones[:, 0:P], pattern=pattern, compare_op=op, fill=0.0,
                                   base=base, channel_multiplier=mult).then_inc(s_const, 1)
            pool.memset(epsc[:, :], EPS).then_inc(s_const, 1)

            last_node = pool.to_reg(N - 1)
            last_edge = pool.to_reg(E - 1)

            done = pool.alloc_register("chunk_count")
            ahead = pool.alloc_register("gathered_count")
            pool.reg_mov(done, 0)
            pool.reg_mov(ahead, R)

            def gather(k, n, used=False):
                pool.wait_ge(s_start, 1)
                pool.wait_ge(s_gidx, n)
                if used:
                    pool.wait_ge(s_h, done)
                pool.indirect_dma_start(xg[:, k, :], None, x, bass.IndirectOffsetOnAxis(ap=gidx[:, k:k + 1], axis=0),
                                        bounds_check=last_node, oob_is_err=False).then_inc(s_gat[k], 16)

            def scatter(k):
                pool.wait_ge(s_start, 1)
                pool.wait_ge(s_sidx, done)
                pool.wait_ge(s_keys, done)
                pool.wait_ge(s_yb, done)
                pool.indirect_dma_start(y_dram[:, :], bass.IndirectOffsetOnAxis(ap=sidx[:, k:k + 1], axis=0),
                                        yb[:, k, :], None, bounds_check=last_edge, oob_is_err=False
                                        ).then_inc(s_sc[k], 16)

            for k in range(R):
                gather(k, k + 1)
            with pool.Fori(0, NCH // R - 1):
                for k in range(R):
                    pool.reg_add(done, done, 1)
                    pool.reg_add(ahead, ahead, 1)
                    gather(k, ahead, True)
                    scatter(k)
            for k in range(R):
                pool.reg_add(done, done, 1)
                scatter(k)

            for n in range(2):
                pool.wait_ge(s_out[n], 16 * NS // 2)
            for k in range(R):
                pool.wait_ge(s_sc[k], 16 * NCH // R)
            most = pool.value_load(big_i[0:1, 0:1], min_val=0, max_val=E)
            with pool.If(most > WIN):
                with pool.Fori(0, NB) as bk:
                    size = pool.value_load(bcnt_i[0:1, bass.ds(bk, 1)], min_val=0, max_val=E)
                    start = pool.value_load(bstart_i[0:1, bass.ds(bk, 1)], min_val=0, max_val=E)
                    end = pool.value_load(bend_i[0:1, bass.ds(bk, 1)], min_val=0, max_val=E)
                    with pool.If(size > WIN):
                        with pool.Fori(start, end) as e:
                            add_edge(pool, bk, e)
                        pool.nop()
                    pool.nop()
                pool.nop()
            pool.nop()

        @block.vector
        def _(v):
            for t, val in ((ones16, 1.0), (onesf, 1.0), (zeros16, 0.0), (xg, 0.0), (gidx, 0), (sidx, 0),
                           (yb, 0.0)):
                v.memset(t[:], val).then_inc(s_init, 1)
            v.memset(bucket_f[:, TILES:TILES + 1], 0.0).then_inc(s_init, 1)
            v.memset(zrow[:, :], 0.0).then_inc(s_zrow, 1)
            v.memset(gkey[:, :], -1.0).then_inc(s_init, 1)
            v.memset(minus1[:, :], -1.0).then_inc(s_init, 1)

            steps = [0]

            def link(ins):
                steps[0] += 1
                ins.then_inc(s_set, 1)
                v.wait_ge(s_set, steps[0])

            v.wait_ge(s_load, 48)
            S, Dn, Ty = src_i[0:EP, :], dst_i[0:EP, :], typ_i[0:EP, :]
            A, B, C, F = (t[0:EP, :] for t in t_i)
            link(v.tensor_scalar(A, S, 9, 2, ALU.arith_shift_right, ALU.logical_shift_left))
            link(v.tensor_scalar(B, S, 3, None, ALU.bitwise_and))
            link(v.tensor_tensor(C, A, B, ALU.bitwise_or))
            link(v.tensor_copy(bucket_f[0:EP, 0:TILES], C))
            link(v.tensor_copy(sub_f[0:EP, :], B))
            link(v.tensor_scalar(B, S, 9, None, ALU.arith_shift_right))
            link(v.tensor_copy(super_f[0:EP, :], B))
            v.wait_ge(s_const, CONSTS)
            link(v.tensor_tensor(is_sub[0:EP, :, :], sub_f[0:EP, :].unsqueeze(2).to_broadcast([EP, TILES, 4]),
                                 iota_f[0:EP, 0:4].unsqueeze(1).to_broadcast([EP, TILES, 4]), ALU.is_equal))

            def count(i, first=False):
                for k in range(U):
                    if not first:
                        v.wait_ge(s_hmm, i * U + k - U + 1)
                    v.tensor_scalar(oh[0:EP, k, 0:NS], iota_b[0:EP, 0:NS], super_f[0:EP, bass.ds(i * U + k, 1)], None,
                                    ALU.is_equal).then_inc(s_hoh, 1)

            count(0, True)
            with v.Fori(1, TILES // U) as i:
                count(i)
            v.wait_ge(s_hmm, TILES)
            v.tensor_copy(hist[0:NS, :], pP[0:NS, 0:4]).then_inc(s_hrow, 1)

            link(v.tensor_scalar(A, S, 2, P - 1, ALU.arith_shift_right, ALU.bitwise_and))
            link(v.tensor_scalar(B, Ty, 7, None, ALU.logical_shift_left))
            link(v.tensor_tensor(C, A, B, ALU.bitwise_or))
            link(v.tensor_copy(keys[0:EP, :], C))
            link(v.tensor_scalar(typ_f[0:EP, :], bucket_f[0:EP, 0:TILES], 1024.0, None, ALU.mult))
            v.wait_ge(s_init, INITS)
            link(v.tensor_tensor(gkey[0:EP, 0:TILES], typ_f[0:EP, :], C, ALU.add))
            link(v.tensor_scalar(bkey[:, :], iota_b[:, :], 1024.0, None, ALU.mult))
            link(v.tensor_scalar(A, Dn, SENT, None, ALU.bitwise_xor))
            link(v.tensor_scalar(B, A, 2047, None, ALU.bitwise_and))
            link(v.tensor_copy(lows[0:EP, :, 0], B))
            link(v.tensor_scalar(F, A, 11, 5, ALU.arith_shift_right, ALU.logical_shift_left))
            link(v.tensor_copy(highs[0:EP, :], F))
            link(v.tensor_copy(typ_f[0:EP, :], Ty))
            for t in range(T):
                v.tensor_scalar(is_type[0:EP, t, :], typ_f[0:EP, :], float(t), None, ALU.is_equal).then_inc(s_set, 1)
            steps[0] += T
            v.wait_ge(s_set, steps[0])
            for t in range(T):
                for g in range(GROUPS):
                    c = slice(g * TG, (g + 1) * TG)
                    v.tensor_tensor_scan(run_type[0:EP, t, c], onesf[0:EP, 0:TG], is_type[0:EP, t, c], 0.0,
                                         ALU.mult, ALU.add).then_inc(s_set, 1)
            steps[0] += T * GROUPS
            v.wait_ge(s_set, steps[0])
            v.tensor_copy(tot[0:EP, 0, :].rearrange("p (t g) -> p t g", g=GROUPS),
                          run_type[0:EP, :, :].rearrange("p t (g j) -> p t g j", g=GROUPS)[:, :, :, TG - 1]
                          ).then_inc(s_rowcnt, 1)
            v.wait_ge(s_base, 1)
            NTG = T * GROUPS
            link(v.tensor_copy(tot[:, 1:3, :].rearrange("p a b -> p (a b)"), pM[:, 0:2 * NTG]))
            link(v.tensor_scalar(tot_i[:, 0, :], tot[:, 2, :], float(P - 1), None, ALU.add))
            link(v.tensor_scalar(tot_i[:, 1, :], tot_i[:, 0, :], 7, None, ALU.arith_shift_right))
            link(v.tensor_copy(nch[:, :, :], tot_i[:, 1, :].rearrange("p (t g) -> p g t", g=GROUPS)))
            for g in range(GROUPS):
                link(v.tensor_tensor_scan(cend[:, g, :], onesf[:, 0:T], nch[:, g, :], 0.0, ALU.mult, ALU.add))
            link(v.tensor_tensor(nch[:, :, :], cend[:, :, :], nch[:, :, :], ALU.subtract))
            link(v.scalar_tensor_tensor(slotbase[0:EP, :, :], nch[0:EP, :, :].rearrange("p g t -> p t g"), float(P),
                                        tot[0:EP, 1, :].rearrange("p (t g) -> p t g", g=GROUPS), ALU.mult, ALU.add))
            for t in range(T):
                v.tensor_tensor(run_type[0:EP, t, :].rearrange("p (g j) -> p g j", g=GROUPS),
                                run_type[0:EP, t, :].rearrange("p (g j) -> p g j", g=GROUPS),
                                slotbase[0:EP, t, :].unsqueeze(2).to_broadcast([EP, GROUPS, TG]),
                                ALU.add).then_inc(s_set, 1)
            steps[0] += T
            v.wait_ge(s_set, steps[0])
            link(v.tensor_tensor(run_type[0:EP, :, :], run_type[0:EP, :, :], is_type[0:EP, :, :], ALU.mult))
            link(v.tensor_reduce(typ_f[0:EP, :], run_type[0:EP, :, :].rearrange("p t j -> p j t"), AX.X, ALU.add))
            link(v.tensor_scalar(A, typ_f[0:EP, :], -1.0, None, ALU.add))
            link(v.tensor_scalar(B, A, P - 1, None, ALU.bitwise_and))
            link(v.tensor_scalar(C, A, 7, None, ALU.arith_shift_right))
            link(v.tensor_copy(slot_lo[0:EP, :], B))
            link(v.tensor_copy(slot_hi[0:EP, :], C))
            for g in range(GROUPS):
                v.tensor_tensor(ctyp_w[:, g, :, :], iota_f[:, 0:CH].unsqueeze(2).to_broadcast([P, CH, T]),
                                cend[:, g, :].unsqueeze(1).to_broadcast([P, CH, T]), ALU.is_ge).then_inc(s_set, 1)
            steps[0] += GROUPS
            v.wait_ge(s_set, steps[0])
            link(v.tensor_reduce(ctyp_f[:, :], ctyp_w[:, :, :, :].rearrange("p g c t -> p (g c) t"), AX.X, ALU.add))
            link(v.tensor_scalar(ctyp_i[:, :], ctyp_f[:, :], float(T - 1), None, ALU.min))
            v.wait_ge(s_hrow, 2)
            link(v.tensor_copy(bcnt[:, :].rearrange("p (s w) -> p w s", w=4),
                               pP[:, 0:4 * NS].rearrange("p (w s) -> p w s", w=4)))
            link(v.tensor_tensor_scan(bend[:, :], onesf[:, 0:NB], bcnt[:, :], 0.0, ALU.mult, ALU.add))
            link(v.tensor_tensor(bstart[:, :], bend[:, :], bcnt[:, :], ALU.subtract))
            link(v.tensor_copy(bstart_i[:, :], bstart[:, :]))
            link(v.tensor_scalar(bfit[:, :], bcnt[:, :], float(WIN), None, ALU.is_le))
            link(v.tensor_copy(bcnt_i[:, :], bcnt[:, :]))
            link(v.tensor_copy(bend_i[:, :], bend[:, :]))
            link(v.tensor_reduce(big[:, :], bcnt[:, :], AX.X, ALU.max))
            link(v.tensor_copy(big_i[:, :], big[:, :]))
            v.tensor_tensor(blen[:, :], bcnt[:, :], bfit[:, :], ALU.mult).then_inc(s_start, 1)
            v.wait_ge(s_start, 1)

            def rank_hot(n, k, first=False):
                if not first:
                    v.wait_ge(s_run, n - U + 1)
                v.tensor_scalar(oh[0:EP, k, :], iota_b[0:EP, :], bucket_f[0:EP, bass.ds(n, 1)], None,
                                ALU.is_equal).then_inc(s_oh, 1)

            def rank_read(n, k):
                v.wait_ge(s_pre, n + 1)
                v.tensor_tensor_reduce(junk[0:EP, :], oh[0:EP, k, :], pP[0:EP, 0:NB], 1.0, 0.0, ALU.mult, ALU.add,
                                       pos4[0:EP, k:k + 1]).then_inc(s_rank, 1)

            def rank_split(m):
                v.wait_ge(s_rank, m * U + U)
                v.tensor_scalar(pos4_i[0:EP, 0, :], pos4[0:EP, :], -1.0, float(SENT), ALU.mult, ALU.add
                                ).then_inc(s_small, 1)
                v.wait_ge(s_small, m * 5 + 1)
                v.tensor_scalar(pos4_i[0:EP, 1, :], pos4_i[0:EP, 0, :], 2047, None, ALU.bitwise_and
                                ).then_inc(s_small, 1)
                v.tensor_scalar(pos4_i[0:EP, 2, :], pos4_i[0:EP, 0, :], 11, None, ALU.arith_shift_right
                                ).then_inc(s_small, 1)
                v.wait_ge(s_small, m * 5 + 3)
                v.tensor_copy(lows[0:EP, bass.ds(m * U, U), 1], pos4_i[0:EP, 1, :]).then_inc(s_small, 1)
                v.tensor_tensor(highs[0:EP, bass.ds(m * U, U)], highs[0:EP, bass.ds(m * U, U)],
                                pos4_i[0:EP, 2, :], ALU.add).then_inc(s_small, 1)

            def perm_hot(n, k, first):
                if not first:
                    v.wait_ge(s_perm, n - U + 1)
                v.tensor_scalar(ohhi[0:EP, k, :], iota_b[0:EP, 0:CH], slot_hi[0:EP, bass.ds(n, 1)], None,
                                ALU.is_equal).then_inc(s_hi, 1)
                v.tensor_scalar(ohlo[0:EP, k, :], iota_b[0:EP, 0:P], slot_lo[0:EP, bass.ds(n, 1)], None,
                                ALU.is_equal).then_inc(s_lo, 1)

            def perm_vals(n, k, small):
                if k == 0:
                    v.wait_ge(s_small, small)
                v.wait_ge(s_hi, n + 1)
                v.tensor_tensor(vals[0:EP, k, 0:2, :], ohhi[0:EP, k, :].unsqueeze(1).to_broadcast([EP, 2, CH]),
                                lows[0:EP, bass.ds(n, 1), :].rearrange("p a b -> p (a b)")
                                .unsqueeze(2).to_broadcast([EP, 2, CH]), ALU.mult).then_inc(s_val, 1)

            def tables(g):
                v.wait_ge(s_perm, (g + 1) * TG)
                v.tensor_copy(m_i[:, :, :].rearrange("p a c -> p (a c)"), pM[:, 0:4 * CH]).then_inc(s_tab, 1)
                n = g * TABS
                c = bass.ds(g * CH, CH)
                v.wait_ge(s_tab, n + 1)
                v.tensor_copy(key_t[:, c], m_i[:, 3, :]).then_inc(s_tab, 1)
                v.tensor_scalar(m2_i[:, 0, :], m_i[:, 2, :], 5, 11, ALU.arith_shift_right, ALU.logical_shift_left
                                ).then_inc(s_tab, 1)
                v.tensor_scalar(m2_i[:, 1, :], m_i[:, 2, :], 31, 11, ALU.bitwise_and, ALU.logical_shift_left
                                ).then_inc(s_tab, 1)
                v.wait_ge(s_tab, n + 4)
                v.tensor_tensor(m2_i[:, 2, :], m2_i[:, 0, :], m_i[:, 0, :], ALU.bitwise_or).then_inc(s_tab, 1)
                v.tensor_tensor(m2_i[:, 3, :], m2_i[:, 1, :], m_i[:, 1, :], ALU.bitwise_or).then_inc(s_tab, 1)
                v.wait_ge(s_tab, n + 6)
                v.tensor_scalar(dst_t[:, c], m2_i[:, 2, :], SENT, None, ALU.bitwise_xor).then_inc(s_tab, 1)
                v.tensor_scalar(pos_t[:, c], m2_i[:, 3, :], SENT, None, ALU.bitwise_xor).then_inc(s_tab, 1)

            stats_end = v.alloc_register("stats_count")
            v.reg_mov(stats_end, 0)

            def stats(q, k, b):
                j = b % 2 * U + k
                v.wait_ge(s_gat[j], q * (16 // 2) + (16 if b % 2 == 0 else 8))
                v.bn_stats(st[:, j, :], xg[:, j, :]).then_inc(s_st, 1)

            def means(q, b):
                v.reg_add(stats_end, stats_end, U)
                v.wait_ge(s_start, 1)
                v.wait_ge(s_st, stats_end)
                for k in range(U):
                    j = b % 2 * U + k
                    v.bn_aggr(mv[:, j, :], st[:, j, :]).then_inc(s_mv, 1)
                v.wait_ge(s_mv, q * U + U)
                j = b % 2 * U
                v.tensor_scalar(nm[:, j:j + U], mv[:, j:j + U, 0], -1.0, None, ALU.mult).then_inc(s_nm, 1)

            def inverse(q, b):
                v.wait_ge(s_sd, q + 1)
                j = b % 2 * U
                v.reciprocal(rstd[:, j:j + U], sd[:, j:j + U]).then_inc(s_rstd, 1)

            def batch(q, b, m, rank, perm, tab=None, first_rank=False, first_perm=False, last=False):
                if b is not None:
                    inverse(q, b)
                for k in range(U):
                    if b is not None and not (last and (b == 1 or k == U - 1)):
                        if k < U - 1:
                            stats(q + 1, k + 1, b + 1)
                        if k == U - 2:
                            means(q + 1, b + 1)
                        if k == U - 1:
                            stats(q + 2, 0, b)
                    if perm:
                        perm_hot((m - 1) * U + k, k, first_perm)
                    if rank:
                        rank_read(m * U + k, k)
                        rank_hot(m * U + k + 1, (k + 1) % U, first_rank and k + 1 < U)
                    if perm:
                        perm_vals((m - 1) * U + k, k, m * 5)
                if rank:
                    rank_split(m)
                if tab is not None:
                    tables(tab)

            rank_hot(0, 0, True)
            batch(None, None, 0, True, False, first_rank=True)
            batch(None, None, 1, True, True, first_perm=True)
            with v.Fori(2, RB) as m:
                batch(None, None, m, True, True)
            batch(None, None, RB, False, True, tab=0)
            batch(None, None, RB, True, False)
            with v.Fori(1, AHEAD) as i:
                batch(None, None, i + RB, True, True)

            for k in range(U):
                stats(0, k, 0)
            means(0, 0)
            stats(1, 0, 1)

            def turn(q, items, first=False, last=False, tabs=None):
                for b, (m, rank, perm, tab, _) in enumerate(items):
                    batch(q + b, b, m, rank, perm, tab, last=last)

            schedule(v, turn)

            def windows(s, j, waited, first=False):
                q, par = slice(0, WIN_P), j % 2
                v.wait_ge(s_win[j], waited)
                key = yw[q, j, :, :].rearrange("p w (r c) -> p w r c", r=WIN_R)[:, :, :, D]
                b4 = blen[q, bass.ds(s * 4, 4)].unsqueeze(2).to_broadcast([WIN_P, 4, WIN_R])
                r4 = rowidx[q, :].unsqueeze(1).to_broadcast([WIN_P, 4, WIN_R])
                v.tensor_tensor(ge[q, par, :, :], r4, b4, ALU.is_ge).then_inc(s_key, 1)
                v.tensor_copy(key_i[q, par, 0, :, :], key).then_inc(s_key, 1)
                v.wait_ge(s_key, s * KEYS + 2)
                v.scalar_tensor_tensor(keym[q, par, :, :], ge[q, par, :, :], float(MASKED), key, ALU.mult, ALU.max
                                       ).then_inc(s_key, 1)
                v.tensor_scalar(key_i[q, par, 1, :, :], key_i[q, par, 0, :, :], P - 1, None, ALU.bitwise_and
                                ).then_inc(s_key, 1)
                v.wait_ge(s_key, s * KEYS + 4)
                v.scalar_tensor_tensor(local[q, par, :, :], ge[q, par, :, :], float(P), key_i[q, par, 1, :, :],
                                       ALU.mult, ALU.add).then_inc(s_wgt, 1)

            def selections(s, j, first=False):
                q, par = slice(0, WIN_P), j % 2
                v.wait_ge(s_krowh, s + 1)
                v.wait_ge(s_krow, s + 1)
                for w in range(4):
                    for r in range(WIN_R):
                        a = w * WIN_R + r
                        v.tensor_scalar(junkc[q, a, :], krow[q, par, w * WIN:(w + 1) * WIN],
                                        keym[q, par, w, r:r + 1], 0.0, ALU.is_equal, ALU.add,
                                        accum_out=cnt[q, par, a:a + 1]).then_inc(s_cnt, 1)
                v.wait_ge(s_cnt, s * 8 + 8)
                v.reciprocal(wgt[q, par, :], cnt[q, par, :]).then_inc(s_inv, 1)
                v.wait_ge(s_inv, s + 1)
                v.wait_ge(s_wgt, s + 1)
                if not first:
                    v.wait_ge(s_sum, s * 4 - 4)
                for w in range(4):
                    for r in range(WIN_R):
                        a = w * WIN_R + r
                        v.tensor_scalar(sel[q, par, a, :], iota_f[q, :], local[q, par, w, r:r + 1],
                                        wgt[q, par, a:a + 1], ALU.is_equal, ALU.mult).then_inc(s_sel, 1)

            windows(0, 0, LOADS)
            for j in range(RS):
                if j + 1 < RS:
                    windows(j + 1, j + 1, LOADS)
                else:
                    windows(RS, 0, 2 * LOADS)
                selections(j, j, first=j < 2)
            with v.Fori(1, NS // RS) as t:
                for j in range(RS):
                    if j + 1 < RS:
                        windows(t * RS + j + 1, j + 1, t * LOADS + LOADS)
                    else:
                        windows(t * RS + RS, 0, t * LOADS + 2 * LOADS)
                    selections(t * RS + j, j)
            windows(NS - 1, 1, (NS // RS + 1) * LOADS)
            selections(NS - 2, 0)
            selections(NS - 1, 1)

        @block.tensor
        def _(pe):
            def mm(o, a, b, **k):
                return pe.matmul(o, a, b, skip_group_check=True, **k)

            pe.wait_ge(s_const, CONSTS)
            pe.wait_ge(s_init, INITS)

            def count(i, first=False):
                for k in range(U):
                    pe.wait_ge(s_hoh, i * U + k + 1)
                    mm(pP[0:NS, 0:4], oh[0:EP, k, 0:NS],
                       is_sub[0:EP, bass.ds(i * U + k, 1), :].rearrange("p a b -> p (a b)"),
                       start=first and k == 0, stop=True).then_inc(s_hmm, 1)

            count(0, True)
            with pe.Fori(1, TILES // U) as i:
                count(i)
            pe.wait_ge(s_hrow, 1)
            for w in range(4):
                t = mm(pP[:, w * NS:(w + 1) * NS], hist[0:NS, w:w + 1].to_broadcast([NS, P]), identf[0:NS, 0:NS],
                       start=True, stop=True)
            t.then_inc(s_hrow, 1)

            NTG = T * GROUPS
            pe.wait_ge(s_rowcnt, 1)
            mm(pM[:, 0:NTG], beforef[0:EP, :], tot[0:EP, 0, :], start=True, stop=True)
            mm(pM[:, NTG:2 * NTG], onesf[0:EP, 0:P], tot[0:EP, 0, :], start=True, stop=True).then_inc(s_base, 1)
            pe.wait_ge(s_start, 1)
            mm(pP[0:EP, 0:NB], onesf[0:1, 0:EP], bstart[0:1, :], start=True, stop=True)

            def rank_in_tile(n, k):
                pe.wait_ge(s_oh, n + 1)
                mm(pP[0:EP, 0:NB], before16[0:EP, 0:EP], oh[0:EP, k, :], start=False, stop=True).then_inc(s_pre, 1)

            def rank_rest(n, k):
                pe.wait_ge(s_rank, n + 1)
                mm(pP[0:EP, 0:NB], notbefore16[0:EP, 0:EP], oh[0:EP, k, :], start=False, stop=True
                   ).then_inc(s_run, 1)

            def permute(n, k):
                pe.wait_ge(s_lo, n + 1)
                pe.wait_ge(s_val, n + 1)
                pe.wait_ge(s_vala, n * 2 + 2)
                mm(pM[:, 0:4 * CH], ohlo[0:EP, k, :], vals[0:EP, k, :, :].rearrange("p a c -> p (a c)"),
                   start=False, stop=True).then_inc(s_perm, 1)

            def clear_slots(g=None):
                if g is not None:
                    pe.wait_ge(s_tab, g * TABS + 1)
                mm(pM[:, 0:4 * CH], zeros16[0:EP, 0:P], zeros16[0:EP, 0:4 * CH], start=True, stop=True)

            def transposes(c, j):
                pe.wait_ge(s_h, c + 1)
                for b in range(KB):
                    t = pe.transpose(pT[j % 2][:, b * P:(b + 1) * P], h[:, j % 4, b * P:(b + 1) * P], identf[:, :])
                t.then_inc(s_tp, 1)

            def product(c, j, typ, first):
                pe.wait_ge(s_hT, c + 1)
                if not first:
                    pe.wait_ge(s_yb, c - 1)
                for b in range(KB):
                    t = mm(pY[j % 2][:, 0:D], hT[:, j % 4, b * P:(b + 1) * P],
                           W[:, b, bass.ds(typ, 1), :].rearrange("p a d -> p (a d)"), start=b == 0, stop=b == KB - 1)
                t.then_inc(s_y, 1)

            def prep(m, rank, perm):
                for k in range(U):
                    if rank:
                        rank_in_tile(m * U + k, k)
                        rank_rest(m * U + k, k)
                    if perm:
                        permute((m - 1) * U + k, k)

            prep(0, True, False)
            clear_slots()
            with pe.Fori(1, RB) as m:
                prep(m, True, True)
            prep(RB, False, True)
            prep(RB, True, False)
            clear_slots(0)
            with pe.Fori(1, AHEAD) as i:
                prep(i + RB, True, True)
            pe.wait_ge(s_w, 16 * KB)
            transposes(0, 0)

            def turn(q, items, first=False, last=False, tabs=None):
                types = [pe.value_load(ctyp_i[0:1, bass.ds(q * U + j, 1)], min_val=0, max_val=T - 1)
                         for j in range(R)]
                for b, (m, rank, perm, _, clear) in enumerate(items):
                    for k in range(U):
                        j = b * U + k
                        c = q * U + j
                        if rank:
                            rank_in_tile(m * U + k, k)
                        if not (last and j == R - 1):
                            transposes(c + 1, j + 1)
                        product(c, j, types[j], first and j < 2)
                        if rank:
                            rank_rest(m * U + k, k)
                        if perm:
                            permute((m - 1) * U + k, k)
                    if clear is not None:
                        clear_slots(clear)

            schedule(pe, turn)

            def key_rows(s, j, first=False):
                pe.wait_ge(s_key, s * KEYS + 3)
                if not first:
                    pe.wait_ge(s_krowh, s)
                    pe.wait_ge(s_krow, s)
                for w in range(4):
                    for r in range(WIN_R):
                        o = (w % 2) * WIN + r * WIN_P
                        t = mm(pK[:, w // 2, o:o + WIN_P],
                               keym[0:WIN_P, j % 2, w, r:r + 1].to_broadcast([WIN_P, P]),
                               ident16[0:WIN_P, 0:WIN_P], start=True, stop=True)
                t.then_inc(s_kbc, 1)

            def sums(s, j, first=False, parts=P):
                for w in range(4):
                    if not first:
                        pe.wait_ge(s_fin, s * 4 + w - 3)
                    else:
                        pe.wait_ge(s_win[j], LOADS)
                    mm(pS[w][0:parts, 0:D], identf[0:parts, 0:parts], xs[0:parts, j, w * D:(w + 1) * D],
                       start=True, stop=False)
                    pe.wait_ge(s_sel, s * 8 + w * 2 + 2)
                    for r in range(WIN_R):
                        a = w * WIN_R + r
                        t = mm(pS[w][0:parts, 0:D], sel[0:WIN_P, j % 2, a, 0:parts],
                               yw[0:WIN_P, j, w, r * ROW:r * ROW + D], start=False, stop=r == WIN_R - 1)
                    t.then_inc(s_sum, 1)

            key_rows(0, 0, True)
            for j in range(RS):
                key_rows(j + 1, (j + 1) % RS)
                sums(j, j, first=j < 1)
            with pe.Fori(1, NS // RS) as t:
                for j in range(RS):
                    key_rows(t * RS + j + 1, (j + 1) % RS)
                    sums(t * RS + j, j)
            key_rows(NS - 1, 1)
            sums(NS - 2, 0)
            sums(NS - 1, 1, parts=LASTP)

        @block.scalar
        def _(act):
            act.wait_ge(s_const, CONSTS)

            def high_vals(n, k, small):
                if k == 0:
                    act.wait_ge(s_small, small)
                act.wait_ge(s_hi, n + 1)
                for a, t in ((2, highs), (3, keys)):
                    act.activation(vals[0:EP, k, a, :], ohhi[0:EP, k, :], ACT.Copy,
                                   scale=t[0:EP, bass.ds(n, 1)]).then_inc(s_vala, 1)

            def gather_index(c, j):
                act.activation(gidx[:, j:j + 1], dst_t[:, bass.ds(c, 1)], ACT.Copy).then_inc(s_gidx, 1)

            def scatter_index(c, j):
                act.activation(sidx[:, j:j + 1], pos_t[:, bass.ds(c, 1)], ACT.Copy).then_inc(s_sidx, 1)
                act.activation(yb[:, j, D:D + 1], key_t[:, bass.ds(c, 1)], ACT.Copy).then_inc(s_keys, 1)

            def deviation(q, b):
                act.wait_ge(s_mv, q * U + U)
                j = b % 2 * U
                act.activation(sd[:, j:j + U], mv[:, j:j + U, 1], ACT.Sqrt, bias=epsc[:, :]).then_inc(s_sd, 1)

            def centre(c, j, q):
                act.wait_ge(s_nm, q + 1)
                j = j % R
                act.activation(h[:, j % 4, :], xg[:, j, :], ACT.Relu, bias=nm[:, j:j + 1]).then_inc(s_h, 1)

            def transposed(c, j):
                act.wait_ge(s_tp, c + 1)
                act.activation(hT[:, j % 4, :], pT[j % 2][:, 0:D], ACT.Copy).then_inc(s_hT, 1)

            def evacuate(c, j, q):
                act.wait_ge(s_y, c + 1)
                act.wait_ge(s_rstd, q + 1)
                act.activation(yb[:, j, 0:D], pY[j % 2][:, 0:D], ACT.Copy, scale=rstd[:, j:j + 1]).then_inc(s_yb, 1)

            def prep(m):
                for k in range(U):
                    high_vals((m - 1) * U + k, k, m * 5)

            with act.Fori(1, RB + 1) as m:
                prep(m)
            act.wait_ge(s_tab, TABS)
            for j in range(R):
                gather_index(j, j)
            with act.Fori(1, AHEAD) as i:
                prep(i + RB)
            deviation(0, 0)
            centre(0, 0, 0)
            centre(1, 1, 0)
            transposed(0, 0)

            def turn(q, items, first=False, last=False, tabs=None):
                if tabs is not None:
                    act.wait_ge(s_tab, tabs * TABS + TABS)
                for b, (m, _, perm, _, _) in enumerate(items):
                    for k in range(U):
                        j = b * U + k
                        c = q * U + j
                        if not last:
                            act.wait_ge(s_gat[j], q * 8 + 16)
                            gather_index(c + R, j)
                        if not first:
                            act.wait_ge(s_sc[j], q * 8)
                        scatter_index(c, j)
                        if perm:
                            high_vals((m - 1) * U + k, k, m * 5)
                        if not (last and j + 2 >= R):
                            if (j + 2) % U == 0:
                                deviation(q + (j + 2) // U, (j + 2) // U)
                            centre(c + 2, j + 2, q + (j + 2) // U)
                        if not (last and j + 1 >= R):
                            transposed(c + 1, j + 1)
                        evacuate(c, j, q + b)

            schedule(act, turn)

            def key_row(s, j, first=False):
                act.wait_ge(s_kbc, s + 1)
                if not first:
                    act.wait_ge(s_cnt, s * 8 - 8)
                for a in range(2):
                    t = act.activation(krow[0:WIN_P, j % 2, a * 2 * WIN:(a + 1) * 2 * WIN],
                                       pK[0:WIN_P, a, 0:2 * WIN], ACT.Copy)
                    t.then_inc(s_krowh, 1) if a == 0 else t.then_inc(s_krow, 1)

            def finish(s, j, stores, parts=P):
                for w in range(4):
                    act.wait_ge(s_sum, s * 4 + w + 1)
                    if w == 0 and stores is not None:
                        act.wait_ge(s_out[j % 2], stores)
                    act.activation(ob[0:parts, j % 2, w * D:(w + 1) * D], pS[w][0:parts, 0:D], ACT.Copy
                                   ).then_inc(s_fin, 1)
                act.wait_ge(s_fin, s * 4 + 4)
                act.dma_start(out[bass.ds(s * SUP, 4 * parts), :].rearrange("(p w) c -> p (w c)", w=4),
                              ob[0:parts, j % 2, :]).then_inc(s_out[j % 2], 16)

            key_row(0, 0, True)
            for j in range(RS):
                key_row(j + 1, (j + 1) % RS, first=j < 1)
                finish(j, j, None if j < 2 else 16)
            with act.Fori(1, NS // RS) as t:
                for j in range(RS):
                    key_row(t * RS + j + 1, (j + 1) % RS)
                    finish(t * RS + j, j, t * 32 + j // 2 * 16)
            key_row(NS - 1, 1)
            finish(NS - 2, 0, NS // RS * 32)
            finish(NS - 1, 1, NS // RS * 32, LASTP)
            for n in range(2):
                act.wait_ge(s_out[n], 16 * NS // 2)


_INS = ["x", "src", "dst", "edge_type_7", "L0_gnn_weights"]


def kernel(**inputs):
    import numpy as _np
    import concourse.bacc as _bacc
    from concourse import mybir as _mybir
    from concourse.bass_utils import run_bass_kernel_spmd as _run

    nc = _bacc.Bacc("TRN2", target_bir_lowering=False, num_devices=1)
    arrays, args = {}, []
    for name in _INS:
        a = _np.ascontiguousarray(inputs[name])
        arrays[f"in_{name}_dram"] = a
        args.append(nc.dram_tensor(f"in_{name}_dram", a.shape, _mybir.dt.from_np(a.dtype), kind="ExternalInput").ap())
    shape = inputs["x"].shape
    args.append(nc.dram_tensor("out_0_dram", shape, _mybir.dt.float32, kind="ExternalOutput").ap())
    gnn_kernel(nc, *args)
    r = _run(nc, [arrays], core_ids=[0])
    return r.results[0]["out_0_dram"]
```

```python
from contextlib import ExitStack

import concourse.bass as bass
from concourse import mybir


ALU = mybir.AluOpType
ACT = mybir.ActivationFunctionType
AX = mybir.AxisListType
F32 = mybir.dt.float32
F16 = mybir.dt.float16
I32 = mybir.dt.int32

P = 128
EPS = 1e-5
U = 4
R = 2 * U
AHEAD = 3
RS = 6
GROUPS = 4
WIN_P, WIN_R = 88, 2
WIN = WIN_P * WIN_R
ROW = 260
SENT = 65535
MASKED = 1024


def gnn_kernel(nc, x, src, dst, etype, weights, out):
    N, D = x.shape
    E = src.shape[0]
    T = weights.shape[0] // D
    KB = D // P
    EP = 125
    TILES = E // EP
    TG = TILES // GROUPS
    CH = (TG * EP + T * (P - 1)) // P
    NCH = GROUPS * CH
    SUP = 4 * P
    NS = -(-N // SUP)
    NB = 4 * NS
    HL = 16
    HH = -(-NB // HL)
    HT = TILES // 40
    LASTP = (N - (NS - 1) * SUP) // 4
    RB = TG // U
    CB = CH // U
    assert E == EP * TILES and TILES % (2 * HT) == 0 and HH * HL <= 512 and TG % U == 0 and CH % R == 0
    assert 2 * CH <= 512 and NB <= 512 and CB == RB + 1 and (CB - AHEAD - 1) % 2 == 0 and NS % RS == 2
    assert E < SENT and N < SENT and T <= 8 and LASTP * 4 == N - (NS - 1) * SUP

    y_dram = nc.dram_tensor("y_by_position", (E + WIN, ROW), F32, kind="Internal").ap()

    with ExitStack() as ctx:
        def sb(name, shape, dt):
            return ctx.enter_context(nc.sbuf_tensor(name, shape, dt))

        def pb(name, shape, dt=F32):
            return ctx.enter_context(nc.psum_tensor(name, shape, dt))

        def sem(name):
            return ctx.enter_context(nc.semaphore(name))

        iota_b = sb("iota_b", [P, NB], F16)
        iota_f = sb("iota_f", [P, P], F32)
        rowidx = sb("rowidx", [P, WIN_R], F32)
        ones16 = sb("ones16", [P, P], F16)
        onesf = sb("onesf", [P, TILES], F32)
        zeros16 = sb("zeros16", [P, 512], F16)
        before16 = sb("before16", [P, P], F16)
        notbefore16 = sb("notbefore16", [P, P], F16)
        beforef = sb("beforef", [P, P], F32)
        ident16 = sb("ident16", [P, P], F16)
        identf = sb("identf", [P, P], F32)
        zrow = sb("zrow", [P, WIN_R * ROW], F32)
        W = sb("W", [P, KB, T, D], F32)
        epsc = sb("epsc", [P, 1], F32)
        src_i = sb("src_i", [P, TILES], I32)
        dst_i = sb("dst_i", [P, TILES], I32)
        typ_i = sb("typ_i", [P, TILES], I32)
        t_i = [sb(f"t_i{n}", [P, TILES], I32) for n in range(4)]
        typ_f = sb("typ_f", [P, TILES], F32)
        bucket_f = sb("bucket_f", [P, TILES + 1], F32)
        slot_lo = sb("slot_lo", [P, TILES], F32)
        slot_hi = sb("slot_hi", [P, TILES], F32)
        dst_key = sb("dst_key", [P, TILES], F32)
        pos_key = sb("pos_key", [P, TILES], F32)
        YW = RS * 4 * WIN_R * ROW
        space = sb("space", [P, max(YW, 2 * T * TILES + NCH * T)], F32)
        is_type = space[:, 0:T * TILES].rearrange("p (t j) -> p t j", t=T)
        run_type = space[:, T * TILES:2 * T * TILES].rearrange("p (t j) -> p t j", t=T)
        ctyp_w = space[:, 2 * T * TILES:2 * T * TILES + NCH * T].rearrange("p (g c t) -> p g c t", g=GROUPS, c=CH)
        yw = space[:, 0:YW].rearrange("p (n w c) -> p n w c", n=RS, w=4)
        tot = sb("tot", [P, 3, T * GROUPS], F32)
        tot_i = sb("tot_i", [P, 2, T * GROUPS], I32)
        nch = sb("nch", [P, GROUPS, T], F32)
        cend = sb("cend", [P, GROUPS, T], F32)
        slotbase = sb("slotbase", [P, T, GROUPS], F32)
        ctyp_f = sb("ctyp_f", [P, NCH], F32)
        ctyp_i = sb("ctyp_i", [P, NCH], I32)
        bcnt_all = sb("bcnt_all", [P, HH * HL], F32)
        bcnt = bcnt_all[:, 0:NB]
        bend = sb("bend", [P, NB], F32)
        bstart = sb("bstart", [P, NB], F32)
        bstart_i = sb("bstart_i", [P, NB], I32)
        bfit = sb("bfit", [P, NB], F32)
        blen = sb("blen", [P, NB], F32)
        bend_i = sb("bend_i", [P, NB], I32)
        bcnt_i = sb("bcnt_i", [P, NB], I32)
        big = sb("big", [P, 1], F32)
        big_i = sb("big_i", [P, 1], I32)
        GW = 512
        gkey = sb("gkey", [P, GW], F32)
        bkey = sb("bkey", [P, NB], F32)
        okey = sb("okey", [P, 2], F32)
        okey_i = sb("okey_i", [P, 1], I32)
        oeq = sb("oeq", [P, GW], F32)
        ocnt = sb("ocnt", [P, 2], F32)
        minus1 = sb("minus1", [P, 1], F32)
        orow = sb("orow", [P, ROW], F32)
        high_h = sb("high_h", [P, TILES], F16)
        low_h = sb("low_h", [P, TILES], F16)
        hist = sb("hist", [P, HL], F32)
        oh = sb("oh", [P, U, NB], F16)
        ohf = oh[:, :, :].rearrange("p u b -> p (u b)")
        oh_high = ohf[:, 0:2 * HT * HH].rearrange("p (n t s) -> p n t s", n=2, t=HT)
        oh_low = ohf[:, 2 * HT * HH:2 * HT * (HH + HL)].rearrange("p (n t s) -> p n t s", n=2, t=HT)
        junk = sb("junk", [P, NB], F16)
        pos4 = sb("pos4", [P, U], F32)
        ohhi = sb("ohhi", [P, U, CH], F16)
        ohlo = sb("ohlo", [P, U, P], F32)
        vals = sb("vals", [P, U, 2, CH], F32)
        m_i = sb("m_i", [P, 2, CH], I32)
        half_i = sb("half_i", [P, 2, CH], I32)
        dst_t = sb("dst_t", [P, NCH], I32)
        pos_t = sb("pos_t", [P, NCH], I32)
        key_t = sb("key_t", [P, NCH], F32)
        XG, H, YB = R * D, 4 * D, R * ROW
        rows = sb("rows", [P, max(XG + 2 * H + YB, RS * 4 * D)], F32)
        xg = rows[:, 0:XG].rearrange("p (k c) -> p k c", k=R)
        h = rows[:, XG:XG + H].rearrange("p (k c) -> p k c", k=4)
        hT = rows[:, XG + H:XG + 2 * H].rearrange("p (k c) -> p k c", k=4)
        yb = rows[:, XG + 2 * H:XG + 2 * H + YB].rearrange("p (k c) -> p k c", k=R)
        xs = rows[:, 0:RS * 4 * D].rearrange("p (k c) -> p k c", k=RS)
        gidx = sb("gidx", [P, R], I32)
        sidx = sb("sidx", [P, R], I32)
        st = sb("st", [P, R, 6], F32)
        mv = sb("mv", [P, R, 2], F32)
        nm = sb("nm", [P, R], F32)
        sd = sb("sd", [P, R], F32)
        rstd = sb("rstd", [P, R], F32)
        ob = sb("ob", [P, 2, 4 * D], F32)
        ge = sb("ge", [P, 2, 4, WIN_R], F32)
        keym = sb("keym", [P, 2, 4, WIN_R], F16)
        key_i = sb("key_i", [P, 2, 2, 4, WIN_R], I32)
        local = sb("local", [P, 2, 4, WIN_R], F32)
        krow = sb("krow", [P, 2, 4 * WIN], F16)
        cnt = sb("cnt", [P, 2, 4 * WIN_R], F32)
        wgt = sb("wgt", [P, 2, 4 * WIN_R], F32)
        negwgt = sb("negwgt", [P, 2, WIN_R], F32)
        dist = sb("dist", [P, 2, WIN_R, P], F32)
        junkc = sb("junkc", [P, 8, WIN], F16)
        sel = sb("sel", [P, 2, 8, P], F32)

        pP = pb("pP", [P, 512])
        pM = pb("pM", [P, 512])
        pT = [pb(f"pT{n}", [P, 512]) for n in range(2)]
        pY = [pb(f"pY{n}", [P, 512]) for n in range(2)]
        pK = pb("pK", [P, 2, 512])
        pS = [pY, pT]

        s_load = sem("s_load")
        s_w = sem("s_w")
        s_const = sem("s_const")
        s_zrow = sem("s_zrow")
        s_zst = sem("s_zst")
        s_init = sem("s_init")
        s_hoh = sem("s_hoh")
        s_hmm = sem("s_hmm")
        s_set = sem("s_set")
        s_hrow = sem("s_hrow")
        s_rowcnt = sem("s_rowcnt")
        s_base = sem("s_base")
        s_start = sem("s_start")
        s_cend = sem("s_cend")
        s_ctyp = sem("s_ctyp")
        s_buckets = sem("s_buckets")
        s_oh = sem("s_oh")
        s_pre = sem("s_pre")
        s_rank = sem("s_rank")
        s_run = sem("s_run")
        s_small = sem("s_small")
        s_hi = sem("s_hi")
        s_lo = sem("s_lo")
        s_val = sem("s_val")
        s_perm = sem("s_perm")
        s_tab = sem("s_tab")
        s_gidx = sem("s_gidx")
        s_sidx = sem("s_sidx")
        s_keys = sem("s_keys")
        s_gat = [sem(f"s_gat{k}") for k in range(R)]
        s_sc = [sem(f"s_sc{k}") for k in range(R)]
        s_st = sem("s_st")
        s_mv = sem("s_mv")
        s_nm = sem("s_nm")
        s_sd = sem("s_sd")
        s_rstd = sem("s_rstd")
        s_h = sem("s_h")
        s_tp = sem("s_tp")
        s_hT = sem("s_hT")
        s_y = sem("s_y")
        s_yb = sem("s_yb")
        s_win = [sem(f"s_win{n}") for n in range(RS)]
        s_key = sem("s_key")
        s_kbc = sem("s_kbc")
        s_krow = sem("s_krow")
        s_krowh = sem("s_krowh")
        s_cnt = sem("s_cnt")
        s_wgt = sem("s_wgt")
        s_inv = sem("s_inv")
        s_neg = sem("s_neg")
        s_dist = sem("s_dist")
        s_sela = sem("s_sela")
        s_sel = sem("s_sel")
        s_sum = sem("s_sum")
        s_fin = sem("s_fin")
        s_finv = sem("s_finv")
        s_oin = sem("s_oin")
        s_ostep = sem("s_ostep")
        s_oout = sem("s_oout")
        s_out = [sem(f"s_out{n}") for n in range(2)]

        block = ctx.enter_context(nc.Block())
        CONSTS = 9
        INITS = 10
        HALF = 2 * D
        BUCKETS = 7
        KEYS = 4
        LOADS = 80
        TABS = 6

        FIRST, MIDDLE, LAST = 1, 2, 3

        def schedule(eng, turn):
            NONE = (0, False, None, None, None)
            LONE = (CB - AHEAD - 1) // 2

            def plain(m, perm=MIDDLE):
                return [(m, True, perm, None, None), (m + 1, True, MIDDLE, None, None)]

            def seam(g, more):
                q = g * CB + 2 * LONE
                m = g * RB + 2 * RB
                first = (m, False, LAST, g + 1, None)
                turn(q, [first, (m, True, None, None, g + 1) if more else NONE])
                turn(q + 2, plain(m + 1, FIRST) if more else [NONE, NONE], tabs=g + 1)

            turn(0, plain(RB + AHEAD), first=True)
            with eng.Fori(1, LONE) as i:
                turn(i * 2, plain(i * 2 + RB + AHEAD))
            with eng.Fori(0, GROUPS - 2) as g:
                seam(g, True)
                with eng.Fori(0, LONE) as i:
                    turn(g * CB + CB + i * 2, plain(g * RB + 2 * RB + AHEAD + i * 2))
            seam(GROUPS - 2, False)
            with eng.Fori(0, CB // 2 - 1) as i:
                turn(i * 2 + (GROUPS - 1) * CB, [NONE, NONE])
            turn(GROUPS * CB - 2, [NONE, NONE], last=True)

        @block.sync
        def _(sp):
            sp.dma_start(src_i[0:EP, :], src.rearrange("(p j) -> p j", j=TILES)).then_inc(s_load, 16)
            sp.dma_start(typ_i[0:EP, :], etype.rearrange("(p j) -> p j", j=TILES)).then_inc(s_load, 16)
            sp.dma_start(dst_i[0:EP, :], dst.rearrange("(p j) -> p j", j=TILES)).then_inc(s_load, 16)
            wv = weights.rearrange("(t b p) n -> b p t n", b=KB, p=P)
            for b in range(KB):
                sp.dma_start(W[:, b, :, :], wv[b]).then_inc(s_w, 16)
            sp.wait_ge(s_zrow, 1)
            sp.dma_start(y_dram[E:E + WIN, :].rearrange("(p r) c -> p (r c)", r=WIN_R),
                         zrow[0:WIN_P, :]).then_inc(s_zst, 16)
            sp.wait_ge(s_zst, 16)
            sp.wait_ge(s_buckets, BUCKETS)
            for k in range(R):
                sp.wait_ge(s_sc[k], 16 * NCH // R)

            def load(s, j, first, parts=P):
                _, starts = nc.values_load_multi_w_load_instructions(
                    bstart_i[0:1, bass.ds(s * 4, 4)], engines=[mybir.EngineType.SP], min_val=0, max_val=E)
                if not first:
                    sp.wait_ge(s_fin, s - RS + 1)
                    sp.wait_ge(s_finv, s - RS + 1)
                sp.dma_start(xs[0:parts, j, :],
                             x[bass.ds(s * SUP, 4 * parts), :].rearrange("(p w) c -> p (w c)", w=4)
                             ).then_inc(s_win[j], 16)
                for w in range(4):
                    sp.dma_start(yw[0:WIN_P, j, w, :],
                                 y_dram[bass.ds(starts[w], WIN), :].rearrange("(p r) c -> p (r c)", r=WIN_R)
                                 ).then_inc(s_win[j], 16)

            for j in range(RS):
                load(j, j, True)
            with sp.Fori(1, NS // RS) as t:
                for j in range(RS):
                    load(t * RS + j, j, False)
            load(NS - 2, 0, False)
            load(NS - 1, 1, False, LASTP)

        def add_edge(pool, bk, e):
            steps = [0]

            def step(ins):
                steps[0] += 1
                ins.then_inc(s_ostep, 1)
                pool.wait_ge(s_ostep, steps[0])

            pool.dma_start(orow[0:1, :], y_dram[bass.ds(e, 1), :]).then_inc(s_oin, 16)
            pool.dma_start(okey[:, 0:1], y_dram[bass.ds(e, 1), D:D + 1].to_broadcast([P, 1])).then_inc(s_oin, 16)
            pool.wait_ge(s_oin, 32)
            step(pool.tensor_copy(okey_i[:, :], okey[:, 0:1]))
            key = pool.value_load(okey_i[0:1, 0:1], min_val=0, max_val=1023)
            step(pool.tensor_tensor(okey[:, 1:2], okey[:, 0:1], bkey[:, bass.ds(bk, 1)], ALU.add))
            step(pool.tensor_scalar(oeq[:, :], gkey[:, :], okey[:, 1:2], None, ALU.is_equal))
            n = GW
            while n > 1:
                n //= 2
                step(pool.tensor_tensor(oeq[:, 0:n], oeq[:, 0:n], oeq[:, n:2 * n], ALU.add))
            step(pool.partition_all_reduce(ocnt[:, 0:1], oeq[:, 0:1], P, bass.bass_isa.ReduceOp.add))
            step(pool.tensor_tensor(ocnt[:, 1:2], ocnt[:, 0:1], minus1[:, :], ALU.pow))
            step(pool.tensor_scalar(orow[0:1, 0:D], orow[0:1, 0:D], ocnt[0:1, 1:2], None, ALU.mult))
            node = nc.s_assert_within((bk // 4) * SUP + bk % 4 + (key % P) * 4, 0, N - 1)
            pool.dma_start(out[bass.ds(node, 1), :], orow[0:1, 0:D], accum_op=ALU.add).then_inc(s_oout, 16)
            pool.wait_ge(s_oout, 16)
            for s in (s_oin, s_ostep, s_oout):
                pool.sem_clear(s)
            pool.dma_reset()

        @block.gpsimd
        def _(pool):
            small = dict(allow_small_or_imprecise_dtypes=True)
            pool.iota(iota_b[:, :], [[1, NB]], base=0, channel_multiplier=0, **small).then_inc(s_const, 1)
            pool.iota(iota_f[:, :], [[1, P]], base=0, channel_multiplier=0, **small).then_inc(s_const, 1)
            pool.iota(rowidx[:, :], [[1, WIN_R]], base=0, channel_multiplier=WIN_R, **small).then_inc(s_const, 1)
            for t, val in ((xg, 0.0), (gidx, 0), (sidx, 0), (yb, 0.0)):
                pool.memset(t[:], val).then_inc(s_init, 1)
            pool.wait_ge(s_init, INITS)
            for t, ones, pattern, base, mult, op in (
                    (before16, ones16, [[1, P]], 0, -1, ALU.is_gt),
                    (notbefore16, ones16, [[-1, P]], 0, 1, ALU.is_ge),
                    (beforef, onesf, [[1, P]], 0, -1, ALU.is_gt),
                    (ident16, ones16, [[1, P]], 0, -1, ALU.is_equal),
                    (identf, onesf, [[1, P]], 0, -1, ALU.is_equal)):
                pool.affine_select(out=t[:, :], in_=ones[:, 0:P], pattern=pattern, compare_op=op, fill=0.0,
                                   base=base, channel_multiplier=mult).then_inc(s_const, 1)
            pool.memset(epsc[:, :], EPS).then_inc(s_const, 1)

            pool.wait_ge(s_cend, GROUPS)
            for g in range(GROUPS):
                for t in range(T - 1):
                    pool.tensor_scalar(ctyp_w[0:1, g, :, t], iota_f[0:1, 0:CH], cend[0:1, g, t:t + 1], None, ALU.is_ge
                                       ).then_inc(s_ctyp, 1)
            compared = GROUPS * (T - 1)
            pool.wait_ge(s_ctyp, compared)
            ended = ctyp_w[0:1, :, :, :].rearrange("p g c t -> p (g c) t")
            for t in range(1, T - 1):
                pool.tensor_tensor(ctyp_f[0:1, :], ended[:, :, 0] if t == 1 else ctyp_f[0:1, :], ended[:, :, t],
                                   ALU.add).then_inc(s_ctyp, 1)
                pool.wait_ge(s_ctyp, compared + t)
            pool.tensor_copy(ctyp_i[0:1, :], ctyp_f[0:1, :]).then_inc(s_ctyp, 1)

            last_node = pool.to_reg(N - 1)
            last_edge = pool.to_reg(E - 1)

            done = pool.alloc_register("chunk_count")
            ahead = pool.alloc_register("gathered_count")
            pool.reg_mov(done, 0)
            pool.reg_mov(ahead, R)

            def gather(k, n, used=False):
                pool.wait_ge(s_start, 1)
                pool.wait_ge(s_gidx, n)
                if used:
                    pool.wait_ge(s_h, done)
                pool.indirect_dma_start(xg[:, k, :], None, x, bass.IndirectOffsetOnAxis(ap=gidx[:, k:k + 1], axis=0),
                                        bounds_check=last_node, oob_is_err=False).then_inc(s_gat[k], 16)

            def scatter(k):
                pool.wait_ge(s_start, 1)
                pool.wait_ge(s_sidx, done)
                pool.wait_ge(s_keys, done)
                pool.wait_ge(s_yb, done)
                pool.indirect_dma_start(y_dram[:, :], bass.IndirectOffsetOnAxis(ap=sidx[:, k:k + 1], axis=0),
                                        yb[:, k, :], None, bounds_check=last_edge, oob_is_err=False
                                        ).then_inc(s_sc[k], 16)

            for k in range(R):
                gather(k, k + 1)
            with pool.Fori(0, NCH // R - 1):
                for k in range(R):
                    pool.reg_add(done, done, 1)
                    pool.reg_add(ahead, ahead, 1)
                    gather(k, ahead, True)
                    scatter(k)
            for k in range(R):
                pool.reg_add(done, done, 1)
                scatter(k)

            for n in range(2):
                pool.wait_ge(s_out[n], 16 * NS // 2)
            for k in range(R):
                pool.wait_ge(s_sc[k], 16 * NCH // R)
            pool.wait_ge(s_buckets, BUCKETS)
            most = pool.value_load(big_i[0:1, 0:1], min_val=0, max_val=E)
            with pool.If(most > WIN):
                with pool.Fori(0, NB) as bk:
                    size = pool.value_load(bcnt_i[0:1, bass.ds(bk, 1)], min_val=0, max_val=E)
                    start = pool.value_load(bstart_i[0:1, bass.ds(bk, 1)], min_val=0, max_val=E)
                    end = pool.value_load(bend_i[0:1, bass.ds(bk, 1)], min_val=0, max_val=E)
                    with pool.If(size > WIN):
                        with pool.Fori(start, end) as e:
                            add_edge(pool, bk, e)
                        pool.nop()
                    pool.nop()
                pool.nop()
            pool.nop()

        @block.vector
        def _(v):
            for t, val in ((ones16, 1.0), (onesf, 1.0), (zeros16, 0.0)):
                v.memset(t[:], val).then_inc(s_init, 1)
            v.memset(bucket_f[:, TILES:TILES + 1], 0.0).then_inc(s_init, 1)
            v.memset(zrow[:, :], 0.0).then_inc(s_zrow, 1)
            v.memset(gkey[:, :], -1.0).then_inc(s_init, 1)
            v.memset(minus1[:, :], -1.0).then_inc(s_init, 1)

            steps = [0]

            def link(ins):
                steps[0] += 1
                ins.then_inc(s_set, 1)
                v.wait_ge(s_set, steps[0])

            v.wait_ge(s_load, 48)
            S, Dn, Ty = src_i[0:EP, :], dst_i[0:EP, :], typ_i[0:EP, :]
            A, B, C, F = (t[0:EP, :] for t in t_i)
            link(v.tensor_scalar(A, S, 9, 2, ALU.arith_shift_right, ALU.logical_shift_left))
            link(v.tensor_scalar(B, S, 3, None, ALU.bitwise_and))
            link(v.tensor_tensor(C, A, B, ALU.bitwise_or))
            link(v.tensor_copy(bucket_f[0:EP, 0:TILES], C))
            link(v.tensor_scalar(B, C, HL - 1, None, ALU.bitwise_and))
            link(v.tensor_copy(low_h[0:EP, :], B))
            link(v.tensor_scalar(B, C, HL.bit_length() - 1, None, ALU.arith_shift_right))
            link(v.tensor_copy(high_h[0:EP, :], B))
            v.wait_ge(s_const, CONSTS)

            def count(i, first=False):
                for n in range(2):
                    if not first:
                        v.wait_ge(s_hmm, i * 2 + n - 1)
                    for hot, part, size in ((oh_high, high_h, HH), (oh_low, low_h, HL)):
                        v.tensor_tensor(hot[0:EP, n, :, :],
                                        iota_b[0:EP, 0:size].unsqueeze(1).to_broadcast([EP, HT, size]),
                                        part[0:EP, bass.ds((i * 2 + n) * HT, HT)].unsqueeze(2)
                                        .to_broadcast([EP, HT, size]), ALU.is_equal).then_inc(s_hoh, 1)

            count(0, True)
            with v.Fori(1, TILES // (2 * HT)) as i:
                count(i)
            v.wait_ge(s_hmm, TILES // HT)
            v.tensor_copy(hist[0:HH, :], pP[0:HH, 0:HL]).then_inc(s_hrow, 1)

            link(v.tensor_scalar(A, S, 2, P - 1, ALU.arith_shift_right, ALU.bitwise_and))
            link(v.tensor_scalar(B, Ty, 7, None, ALU.logical_shift_left))
            link(v.tensor_tensor(C, A, B, ALU.bitwise_or))
            link(v.tensor_scalar(A, Dn, SENT, 5, ALU.bitwise_xor, ALU.logical_shift_left))
            link(v.tensor_scalar(B, C, 31, None, ALU.bitwise_and))
            link(v.tensor_tensor(dst_key[0:EP, :], A, B, ALU.add))
            link(v.tensor_scalar(F, C, 5, None, ALU.arith_shift_right))
            link(v.tensor_scalar(pos_key[0:EP, :], F, float(SENT * 32), None, ALU.add))
            link(v.tensor_copy(typ_f[0:EP, :], Ty))
            for t in range(T):
                v.tensor_scalar(is_type[0:EP, t, :], typ_f[0:EP, :], float(t), None, ALU.is_equal).then_inc(s_set, 1)
            steps[0] += T
            v.wait_ge(s_set, steps[0])
            for t in range(T):
                for g in range(GROUPS):
                    c = slice(g * TG, (g + 1) * TG)
                    v.tensor_tensor_scan(run_type[0:EP, t, c], onesf[0:EP, 0:TG], is_type[0:EP, t, c], 0.0,
                                         ALU.mult, ALU.add).then_inc(s_set, 1)
            steps[0] += T * GROUPS
            v.wait_ge(s_set, steps[0])
            v.tensor_copy(tot[0:EP, 0, :].rearrange("p (t g) -> p t g", g=GROUPS),
                          run_type[0:EP, :, :].rearrange("p t (g j) -> p t g j", g=GROUPS)[:, :, :, TG - 1]
                          ).then_inc(s_rowcnt, 1)
            v.wait_ge(s_base, 1)
            NTG = T * GROUPS
            link(v.tensor_copy(tot[:, 1:3, :].rearrange("p a b -> p (a b)"), pM[:, 0:2 * NTG]))
            link(v.tensor_scalar(tot_i[:, 0, :], tot[:, 2, :], float(P - 1), None, ALU.add))
            link(v.tensor_scalar(tot_i[:, 1, :], tot_i[:, 0, :], 7, None, ALU.arith_shift_right))
            link(v.tensor_copy(nch[:, :, :], tot_i[:, 1, :].rearrange("p (t g) -> p g t", g=GROUPS)))
            for g in range(GROUPS):
                v.tensor_tensor_scan(cend[:, g, :], onesf[:, 0:T], nch[:, g, :], 0.0, ALU.mult, ALU.add
                                     ).then_inc(s_cend, 1)
            v.wait_ge(s_cend, GROUPS)
            link(v.tensor_tensor(nch[:, :, :], cend[:, :, :], nch[:, :, :], ALU.subtract))
            link(v.scalar_tensor_tensor(slotbase[0:EP, :, :], nch[0:EP, :, :].rearrange("p g t -> p t g"), float(P),
                                        tot[0:EP, 1, :].rearrange("p (t g) -> p t g", g=GROUPS), ALU.mult, ALU.add))
            for t in range(T):
                v.tensor_tensor(run_type[0:EP, t, :].rearrange("p (g j) -> p g j", g=GROUPS),
                                run_type[0:EP, t, :].rearrange("p (g j) -> p g j", g=GROUPS),
                                slotbase[0:EP, t, :].unsqueeze(2).to_broadcast([EP, GROUPS, TG]),
                                ALU.add).then_inc(s_set, 1)
            steps[0] += T
            v.wait_ge(s_set, steps[0])
            link(v.tensor_tensor(run_type[0:EP, :, :], run_type[0:EP, :, :], is_type[0:EP, :, :], ALU.mult))
            link(v.tensor_reduce(typ_f[0:EP, :], run_type[0:EP, :, :].rearrange("p t j -> p j t"), AX.X, ALU.add))
            link(v.tensor_scalar(A, typ_f[0:EP, :], -1.0, None, ALU.add))
            link(v.tensor_scalar(B, A, P - 1, None, ALU.bitwise_and))
            link(v.tensor_scalar(C, A, 7, None, ALU.arith_shift_right))
            link(v.tensor_copy(slot_lo[0:EP, :], B))
            link(v.tensor_copy(slot_hi[0:EP, :], C))
            v.wait_ge(s_hrow, 2)
            link(v.tensor_copy(bcnt_all[:, :].rearrange("p (h l) -> p l h", l=HL),
                               pP[:, 0:HH * HL].rearrange("p (l h) -> p l h", l=HL)))
            link(v.tensor_tensor_scan(bend[:, :], onesf[:, 0:NB], bcnt[:, :], 0.0, ALU.mult, ALU.add))
            v.tensor_tensor(bstart[:, :], bend[:, :], bcnt[:, :], ALU.subtract).then_inc(s_start, 1)
            v.wait_ge(s_start, 1)

            def rank_hot(n, k, first=False):
                if not first:
                    v.wait_ge(s_run, n - U + 1)
                v.tensor_scalar(oh[0:EP, k, :], iota_b[0:EP, :], bucket_f[0:EP, bass.ds(n, 1)], None,
                                ALU.is_equal).then_inc(s_oh, 1)

            def rank_read(n, k):
                v.wait_ge(s_pre, n + 1)
                v.tensor_tensor_reduce(junk[0:EP, :], oh[0:EP, k, :], pP[0:EP, 0:NB], 1.0, 0.0, ALU.mult, ALU.add,
                                       pos4[0:EP, k:k + 1]).then_inc(s_rank, 1)

            def rank_pieces(m):
                v.wait_ge(s_rank, m * U + U)
                c = bass.ds(m * U, U)
                v.scalar_tensor_tensor(pos_key[0:EP, c], pos4[0:EP, :], -32.0, pos_key[0:EP, c], ALU.mult, ALU.add
                                       ).then_inc(s_small, 1)

            def perm_hot(n, k, first):
                if not first:
                    v.wait_ge(s_perm, n - U + 1)
                v.tensor_scalar(ohhi[0:EP, k, :], iota_b[0:EP, 0:CH], slot_hi[0:EP, bass.ds(n, 1)], None,
                                ALU.is_equal).then_inc(s_hi, 1)
                v.tensor_scalar(ohlo[0:EP, k, :], iota_b[0:EP, 0:P], slot_lo[0:EP, bass.ds(n, 1)], None,
                                ALU.is_equal).then_inc(s_lo, 1)

            def tables(g):
                v.wait_ge(s_perm, (g + 1) * TG)
                v.tensor_copy(m_i[:, :, :].rearrange("p a c -> p (a c)"), pM[:, 0:2 * CH]).then_inc(s_tab, 1)
                n = g * TABS
                c = bass.ds(g * CH, CH)
                v.wait_ge(s_tab, n + 1)
                v.tensor_scalar(dst_t[:, c], m_i[:, 0, :], 5, SENT, ALU.arith_shift_right, ALU.bitwise_xor
                                ).then_inc(s_tab, 1)
                v.tensor_scalar(pos_t[:, c], m_i[:, 1, :], 5, SENT, ALU.arith_shift_right, ALU.bitwise_xor
                                ).then_inc(s_tab, 1)
                v.tensor_scalar(half_i[:, 0, :], m_i[:, 0, :], 31, None, ALU.bitwise_and).then_inc(s_tab, 1)
                v.tensor_scalar(half_i[:, 1, :], m_i[:, 1, :], 31, 5, ALU.bitwise_and, ALU.logical_shift_left
                                ).then_inc(s_tab, 1)
                v.wait_ge(s_tab, n + 5)
                v.tensor_tensor(key_t[:, c], half_i[:, 0, :], half_i[:, 1, :], ALU.add).then_inc(s_tab, 1)

            stats_end = v.alloc_register("stats_count")
            v.reg_mov(stats_end, 0)

            def stats(q, k, b):
                j = b % 2 * U + k
                v.wait_ge(s_gat[j], q * (16 // 2) + (16 if b % 2 == 0 else 8))
                v.bn_stats(st[:, j, :], xg[:, j, :]).then_inc(s_st, 1)

            def means(q, b):
                v.reg_add(stats_end, stats_end, U)
                v.wait_ge(s_start, 1)
                v.wait_ge(s_st, stats_end)
                for k in range(U):
                    j = b % 2 * U + k
                    v.bn_aggr(mv[:, j, :], st[:, j, :]).then_inc(s_mv, 1)
                v.wait_ge(s_mv, q * U + U)
                j = b % 2 * U
                v.tensor_scalar(nm[:, j:j + U], mv[:, j:j + U, 0], -1.0, None, ALU.mult).then_inc(s_nm, 1)

            def inverse(q, b):
                v.wait_ge(s_sd, q + 1)
                j = b % 2 * U
                v.reciprocal(rstd[:, j:j + U], sd[:, j:j + U]).then_inc(s_rstd, 1)

            def batch(q, b, m, rank, perm, tab=None, first_rank=False, first_perm=False, last=False):
                if b is not None:
                    inverse(q, b)
                for k in range(U):
                    if b is not None and not (last and (b == 1 or k == U - 1)):
                        if k < U - 1:
                            stats(q + 1, k + 1, b + 1)
                        if k == U - 2:
                            means(q + 1, b + 1)
                        if k == U - 1:
                            stats(q + 2, 0, b)
                    if perm:
                        perm_hot((m - 1) * U + k, k, first_perm)
                    if rank:
                        if k == 0 and not first_rank:
                            v.wait_ge(s_small, m)
                        rank_read(m * U + k, k)
                        rank_hot(m * U + k + 1, (k + 1) % U, first_rank and k + 1 < U)
                if rank:
                    rank_pieces(m)
                if tab is not None:
                    tables(tab)

            rank_hot(0, 0, True)
            batch(None, None, 0, True, False, first_rank=True)
            batch(None, None, 1, True, True, first_perm=True)
            with v.Fori(2, RB) as m:
                batch(None, None, m, True, True)
            batch(None, None, RB, False, True, tab=0)
            batch(None, None, RB, True, False)
            with v.Fori(1, AHEAD) as i:
                batch(None, None, i + RB, True, True)

            for k in range(U):
                stats(0, k, 0)
            means(0, 0)
            stats(1, 0, 1)

            def turn(q, items, first=False, last=False, tabs=None):
                for b, (m, rank, perm, tab, _) in enumerate(items):
                    batch(q + b, b, m, rank, perm, tab, last=last)

            schedule(v, turn)

            link(v.tensor_scalar(bfit[:, :], bcnt[:, :], float(WIN), None, ALU.is_le))
            link(v.tensor_reduce(big[:, :], bcnt[:, :], AX.X, ALU.max))
            link(v.tensor_scalar(A, S, 2, P - 1, ALU.arith_shift_right, ALU.bitwise_and))
            link(v.tensor_scalar(B, Ty, 7, None, ALU.logical_shift_left))
            link(v.tensor_tensor(C, A, B, ALU.bitwise_or))
            link(v.tensor_scalar(typ_f[0:EP, :], bucket_f[0:EP, 0:TILES], 1024.0, None, ALU.mult))
            v.wait_ge(s_init, INITS)
            for t in (v.tensor_tensor(gkey[0:EP, 0:TILES], typ_f[0:EP, :], C, ALU.add),
                      v.tensor_scalar(bkey[:, :], iota_b[:, :], 1024.0, None, ALU.mult),
                      v.tensor_copy(bstart_i[:, :], bstart[:, :]),
                      v.tensor_copy(bcnt_i[:, :], bcnt[:, :]),
                      v.tensor_copy(bend_i[:, :], bend[:, :]),
                      v.tensor_copy(big_i[:, :], big[:, :]),
                      v.tensor_tensor(blen[:, :], bcnt[:, :], bfit[:, :], ALU.mult)):
                t.then_inc(s_buckets, 1)
            v.wait_ge(s_buckets, BUCKETS)

            def windows(s, j, waited, first=False):
                q, par = slice(0, WIN_P), j % 2
                v.wait_ge(s_win[j], waited)
                key = yw[q, j, :, :].rearrange("p w (r c) -> p w r c", r=WIN_R)[:, :, :, D]
                b4 = blen[q, bass.ds(s * 4, 4)].unsqueeze(2).to_broadcast([WIN_P, 4, WIN_R])
                r4 = rowidx[q, :].unsqueeze(1).to_broadcast([WIN_P, 4, WIN_R])
                v.tensor_tensor(ge[q, par, :, :], r4, b4, ALU.is_ge).then_inc(s_key, 1)
                v.tensor_copy(key_i[q, par, 0, :, :], key).then_inc(s_key, 1)
                v.wait_ge(s_key, s * KEYS + 2)
                v.scalar_tensor_tensor(keym[q, par, :, :], ge[q, par, :, :], float(MASKED), key, ALU.mult, ALU.max
                                       ).then_inc(s_key, 1)
                v.tensor_scalar(key_i[q, par, 1, :, :], key_i[q, par, 0, :, :], P - 1, None, ALU.bitwise_and
                                ).then_inc(s_key, 1)
                v.wait_ge(s_key, s * KEYS + 4)
                if not first:
                    v.wait_ge(s_sela, s * 2 - 2)
                v.scalar_tensor_tensor(local[q, par, :, :], ge[q, par, :, :], float(P), key_i[q, par, 1, :, :],
                                       ALU.mult, ALU.add).then_inc(s_wgt, 1)

            def add_x(s, j, stores, parts=P):
                v.wait_ge(s_sum, s * 2 + 2)
                if stores is not None:
                    v.wait_ge(s_out[j % 2], stores)
                v.tensor_tensor(ob[0:parts, j % 2, HALF:], pS[j % 2][1][0:parts, :], xs[0:parts, j, HALF:],
                                ALU.add).then_inc(s_finv, 1)

            def selections(s, j, first=False, before=None):
                q, par = slice(0, WIN_P), j % 2
                v.wait_ge(s_krowh, s + 1)
                v.wait_ge(s_krow, s + 1)
                for w in range(4):
                    for r in range(WIN_R):
                        a = w * WIN_R + r
                        v.tensor_scalar(junkc[q, a, :], krow[q, par, w * WIN:(w + 1) * WIN],
                                        keym[q, par, w, r:r + 1], 0.0, ALU.is_equal, ALU.add,
                                        accum_out=cnt[q, par, a:a + 1]).then_inc(s_cnt, 1)
                v.wait_ge(s_cnt, s * 8 + 8)
                v.reciprocal(wgt[q, par, :], cnt[q, par, :]).then_inc(s_inv, 1)
                v.wait_ge(s_inv, s + 1)
                v.wait_ge(s_wgt, s + 1)
                if not first:
                    v.wait_ge(s_sum, s * 2 - 2)
                v.tensor_scalar(negwgt[q, par, :], wgt[q, par, 3 * WIN_R:], -1.0, None, ALU.mult).then_inc(s_neg, 1)
                for w in range(3):
                    if w == 2 and before is not None:
                        before()
                    for r in range(WIN_R):
                        a = w * WIN_R + r
                        v.tensor_scalar(sel[q, par, a, :], iota_f[q, :], local[q, par, w, r:r + 1],
                                        wgt[q, par, a:a + 1], ALU.is_equal, ALU.mult).then_inc(s_sel, 1)

            windows(0, 0, LOADS, True)
            for j in range(RS):
                if j + 1 < RS:
                    windows(j + 1, j + 1, LOADS, j < 1)
                else:
                    windows(RS, 0, 2 * LOADS)
                stores = None if j < 3 else 16 * ((j - 1) // 2)
                selections(j, j, j < 2, None if j < 1 else lambda: add_x(j - 1, j - 1, stores))
            with v.Fori(1, NS // RS) as t:
                for j in range(RS):
                    if j + 1 < RS:
                        windows(t * RS + j + 1, j + 1, t * LOADS + LOADS)
                    else:
                        windows(t * RS + RS, 0, t * LOADS + 2 * LOADS)
                    i = (j - 1) % RS
                    selections(t * RS + j, j, False,
                               lambda: add_x(t * RS + j - 1, i, t * (RS * 8) + (j - 1) // 2 * 16))
            windows(NS - 1, 1, (NS // RS + 1) * LOADS)
            full = NS // RS * (RS * 8)
            selections(NS - 2, 0, False, lambda: add_x(NS - 3, RS - 1, full - 16))
            selections(NS - 1, 1, False, lambda: add_x(NS - 2, 0, full))
            add_x(NS - 1, 1, full, LASTP)

        @block.tensor
        def _(pe):
            def mm(o, a, b, **k):
                return pe.matmul(o, a, b, skip_group_check=True, **k)

            pe.wait_ge(s_const, CONSTS)
            pe.wait_ge(s_init, INITS)

            def count(i, first=False):
                for n in range(2):
                    pe.wait_ge(s_hoh, i * 4 + n * 2 + 2)
                    for k in range(HT):
                        t = mm(pP[0:HH, 0:HL], oh_high[0:EP, n, k, :], oh_low[0:EP, n, k, :],
                               start=first and n == 0 and k == 0, stop=True)
                    t.then_inc(s_hmm, 1)

            count(0, True)
            with pe.Fori(1, TILES // (2 * HT)) as i:
                count(i)
            pe.wait_ge(s_hrow, 1)
            for w in range(HL):
                t = mm(pP[:, w * HH:(w + 1) * HH], hist[0:HH, w:w + 1].to_broadcast([HH, P]), identf[0:HH, 0:HH],
                       start=True, stop=True)
            t.then_inc(s_hrow, 1)

            NTG = T * GROUPS
            pe.wait_ge(s_rowcnt, 1)
            mm(pM[:, 0:NTG], beforef[0:EP, :], tot[0:EP, 0, :], start=True, stop=True)
            mm(pM[:, NTG:2 * NTG], onesf[0:EP, 0:P], tot[0:EP, 0, :], start=True, stop=True).then_inc(s_base, 1)
            pe.wait_ge(s_start, 1)
            mm(pP[0:EP, 0:NB], onesf[0:1, 0:EP], bstart[0:1, :], start=True, stop=True)

            def rank_in_tile(n, k):
                pe.wait_ge(s_oh, n + 1)
                mm(pP[0:EP, 0:NB], before16[0:EP, 0:EP], oh[0:EP, k, :], start=False, stop=True).then_inc(s_pre, 1)

            def rank_rest(n, k):
                pe.wait_ge(s_rank, n + 1)
                mm(pP[0:EP, 0:NB], notbefore16[0:EP, 0:EP], oh[0:EP, k, :], start=False, stop=True
                   ).then_inc(s_run, 1)

            def permute(n, k):
                pe.wait_ge(s_lo, n + 1)
                pe.wait_ge(s_val, n * 2 + 2)
                mm(pM[:, 0:2 * CH], ohlo[0:EP, k, :], vals[0:EP, k, :, :].rearrange("p a c -> p (a c)"),
                   start=False, stop=True).then_inc(s_perm, 1)

            def clear_slots(g=None):
                if g is not None:
                    pe.wait_ge(s_tab, g * TABS + 1)
                mm(pM[:, 0:2 * CH], zeros16[0:EP, 0:P], zeros16[0:EP, 0:2 * CH], start=True, stop=True)

            def transposes(c, j):
                pe.wait_ge(s_h, c + 1)
                for b in range(KB):
                    t = pe.transpose(pT[j % 2][:, b * P:(b + 1) * P], h[:, j % 4, b * P:(b + 1) * P], identf[:, :])
                t.then_inc(s_tp, 1)

            def product(c, j, typ, first):
                pe.wait_ge(s_hT, c + 1)
                if not first:
                    pe.wait_ge(s_yb, c - 1)
                for b in range(KB):
                    t = mm(pY[j % 2][:, 0:D], hT[:, j % 4, b * P:(b + 1) * P],
                           W[:, b, bass.ds(typ, 1), :].rearrange("p a d -> p (a d)"), start=b == 0, stop=b == KB - 1)
                t.then_inc(s_y, 1)

            def prep_tile(m, k, rank, perm):
                if rank:
                    rank_rest(m * U + k, k)
                    rank_in_tile(m * U + k + 1, (k + 1) % U)
                if perm and (perm != FIRST or k > 0):
                    permute((m - 1) * U + k - 1, (k - 1) % U)
                if perm == LAST and k == U - 1:
                    permute((m - 1) * U + k, k)

            def prep(m, rank, perm):
                for k in range(U):
                    prep_tile(m, k, rank, perm)

            rank_in_tile(0, 0)
            prep(0, True, None)
            clear_slots()
            prep(1, True, FIRST)
            with pe.Fori(2, RB) as m:
                prep(m, True, MIDDLE)
            prep(RB, False, LAST)
            prep(RB, True, None)
            clear_slots(0)
            prep(RB + 1, True, FIRST)
            with pe.Fori(2, AHEAD) as i:
                prep(i + RB, True, MIDDLE)
            pe.wait_ge(s_w, 16 * KB)
            transposes(0, 0)

            def turn(q, items, first=False, last=False, tabs=None):
                _, types = nc.values_load_multi_w_load_instructions(
                    ctyp_i[0:1, bass.ds(q * U, R)], engines=[mybir.EngineType.PE], min_val=0, max_val=T - 1)
                for b, (m, rank, perm, _, clear) in enumerate(items):
                    for k in range(U):
                        j = b * U + k
                        c = q * U + j
                        if not (last and j == R - 1):
                            transposes(c + 1, j + 1)
                        product(c, j, types[j], first and j < 2)
                        prep_tile(m, k, rank, perm)
                    if clear is not None:
                        clear_slots(clear)

            pe.wait_ge(s_ctyp, (GROUPS + 1) * (T - 1))
            schedule(pe, turn)

            def key_rows(s, j, first=False):
                pe.wait_ge(s_key, s * KEYS + 3)
                if not first:
                    pe.wait_ge(s_krowh, s)
                    pe.wait_ge(s_krow, s)
                for w in range(4):
                    for r in range(WIN_R):
                        o = (w % 2) * WIN + r * WIN_P
                        t = mm(pK[:, w // 2, o:o + WIN_P],
                               keym[0:WIN_P, j % 2, w, r:r + 1].to_broadcast([WIN_P, P]),
                               ident16[0:WIN_P, 0:WIN_P], start=True, stop=True)
                t.then_inc(s_kbc, 1)

            def sums(s, j, waited, first=False, parts=P):
                pe.wait_ge(s_win[j], waited)
                for n in range(2):
                    if not first:
                        pe.wait_ge(s_finv if n else s_fin, s - 1)
                    if n == 0:
                        mm(pS[j % 2][n][0:parts, :], identf[0:parts, 0:parts], xs[0:parts, j, 0:HALF],
                           start=True, stop=False)
                    for w in (2 * n, 2 * n + 1):
                        if w < 3:
                            pe.wait_ge(s_sel, s * 6 + w * 2 + 2)
                        else:
                            pe.wait_ge(s_sela, s * 2 + 2)
                        for r in range(WIN_R):
                            t = mm(pS[j % 2][n][0:parts, w % 2 * D:(w % 2 + 1) * D],
                                   sel[0:WIN_P, j % 2, w * WIN_R + r, 0:parts],
                                   yw[0:WIN_P, j, w, r * ROW:r * ROW + D], start=n == 1 and r == 0,
                                   stop=r == WIN_R - 1)
                    t.then_inc(s_sum, 1)

            key_rows(0, 0, True)
            for j in range(RS):
                key_rows(j + 1, (j + 1) % RS)
                sums(j, j, LOADS, first=j < 2)
            with pe.Fori(1, NS // RS) as t:
                for j in range(RS):
                    key_rows(t * RS + j + 1, (j + 1) % RS)
                    sums(t * RS + j, j, t * LOADS + LOADS)
            key_rows(NS - 1, 1)
            sums(NS - 2, 0, (NS // RS + 1) * LOADS)
            sums(NS - 1, 1, (NS // RS + 1) * LOADS, parts=LASTP)

        @block.scalar
        def _(act):
            act.wait_ge(s_const, CONSTS)

            def values(n, k, m):
                if k == 0:
                    act.wait_ge(s_small, m)
                act.wait_ge(s_hi, n + 1)
                for a, t in ((0, dst_key), (1, pos_key)):
                    act.activation(vals[0:EP, k, a, :], ohhi[0:EP, k, :], ACT.Copy,
                                   scale=t[0:EP, bass.ds(n, 1)]).then_inc(s_val, 1)

            def gather_index(c, j):
                act.activation(gidx[:, j:j + 1], dst_t[:, bass.ds(c, 1)], ACT.Copy).then_inc(s_gidx, 1)

            def scatter_index(c, j):
                act.activation(sidx[:, j:j + 1], pos_t[:, bass.ds(c, 1)], ACT.Copy).then_inc(s_sidx, 1)
                act.activation(yb[:, j, D:D + 1], key_t[:, bass.ds(c, 1)], ACT.Copy).then_inc(s_keys, 1)

            def deviation(q, b):
                act.wait_ge(s_mv, q * U + U)
                j = b % 2 * U
                act.activation(sd[:, j:j + U], mv[:, j:j + U, 1], ACT.Sqrt, bias=epsc[:, :]).then_inc(s_sd, 1)

            def centre(c, j, q):
                act.wait_ge(s_nm, q + 1)
                j = j % R
                act.activation(h[:, j % 4, :], xg[:, j, :], ACT.Relu, bias=nm[:, j:j + 1]).then_inc(s_h, 1)

            def transposed(c, j):
                act.wait_ge(s_tp, c + 1)
                act.activation(hT[:, j % 4, :], pT[j % 2][:, 0:D], ACT.Copy).then_inc(s_hT, 1)

            def evacuate(c, j, q):
                act.wait_ge(s_y, c + 1)
                act.wait_ge(s_rstd, q + 1)
                act.activation(yb[:, j, 0:D], pY[j % 2][:, 0:D], ACT.Copy, scale=rstd[:, j:j + 1]).then_inc(s_yb, 1)

            def prep(m):
                for k in range(U):
                    values((m - 1) * U + k, k, m)

            with act.Fori(1, RB + 1) as m:
                prep(m)
            act.wait_ge(s_tab, TABS)
            for j in range(R):
                gather_index(j, j)
            with act.Fori(1, AHEAD) as i:
                prep(i + RB)
            deviation(0, 0)
            centre(0, 0, 0)
            centre(1, 1, 0)
            transposed(0, 0)

            def turn(q, items, first=False, last=False, tabs=None):
                if tabs is not None:
                    act.wait_ge(s_tab, tabs * TABS + TABS)
                for b, (m, _, perm, _, _) in enumerate(items):
                    for k in range(U):
                        j = b * U + k
                        c = q * U + j
                        if not last:
                            act.wait_ge(s_gat[j], q * 8 + 16)
                            gather_index(c + R, j)
                        if not first:
                            act.wait_ge(s_sc[j], q * 8)
                        scatter_index(c, j)
                        if perm:
                            values((m - 1) * U + k, k, m)
                        if not (last and j + 2 >= R):
                            if (j + 2) % U == 0:
                                deviation(q + (j + 2) // U, (j + 2) // U)
                            centre(c + 2, j + 2, q + (j + 2) // U)
                        if not (last and j + 1 >= R):
                            transposed(c + 1, j + 1)
                        evacuate(c, j, q + b)

            schedule(act, turn)

            def key_row(s, j, first=False):
                act.wait_ge(s_kbc, s + 1)
                if not first:
                    act.wait_ge(s_cnt, s * 8 - 8)
                for a in range(2):
                    t = act.activation(krow[0:WIN_P, j % 2, a * 2 * WIN:(a + 1) * 2 * WIN],
                                       pK[0:WIN_P, a, 0:2 * WIN], ACT.Copy)
                    t.then_inc(s_krowh, 1) if a == 0 else t.then_inc(s_krow, 1)

            def selection(s, j, first=False):
                q, par = slice(0, WIN_P), j % 2
                act.wait_ge(s_wgt, s + 1)
                if not first:
                    act.wait_ge(s_sela, s * 2 - 2)
                for r in range(WIN_R):
                    act.activation(dist[q, par, r, :], iota_f[q, :], ACT.Abs, scale=-1.0,
                                   bias=local[q, par, 3, r:r + 1]).then_inc(s_dist, 1)
                act.wait_ge(s_dist, s * 2 + 2)
                act.wait_ge(s_neg, s + 1)
                if not first:
                    act.wait_ge(s_sum, s * 2 - 2)
                for r in range(WIN_R):
                    a = 3 * WIN_R + r
                    act.activation(sel[q, par, a, :], dist[q, par, r, :], ACT.Relu, scale=negwgt[q, par, r:r + 1],
                                   bias=wgt[q, par, a:a + 1]).then_inc(s_sela, 1)

            def finish(s, j, stores, parts=P):
                act.wait_ge(s_sum, s * 2 + 1)
                if stores is not None:
                    act.wait_ge(s_out[j % 2], stores)
                act.activation(ob[0:parts, j % 2, 0:HALF], pS[j % 2][0][0:parts, :], ACT.Copy).then_inc(s_fin, 1)
                act.wait_ge(s_fin, s + 1)
                act.wait_ge(s_finv, s + 1)
                act.dma_start(out[bass.ds(s * SUP, 4 * parts), :].rearrange("(p w) c -> p (w c)", w=4),
                              ob[0:parts, j % 2, :]).then_inc(s_out[j % 2], 16)

            key_row(0, 0, True)
            for j in range(RS):
                key_row(j + 1, (j + 1) % RS, first=j < 1)
                selection(j, j, first=j < 2)
                if j > 0:
                    finish(j - 1, j - 1, None if j < 3 else 16 * ((j - 1) // 2))
            with act.Fori(1, NS // RS) as t:
                for j in range(RS):
                    key_row(t * RS + j + 1, (j + 1) % RS)
                    selection(t * RS + j, j)
                    finish(t * RS + j - 1, (j - 1) % RS, t * (RS * 8) + (j - 1) // 2 * 16)
            full = NS // RS * (RS * 8)
            key_row(NS - 1, 1)
            selection(NS - 2, 0)
            finish(NS - 3, RS - 1, full - 16)
            selection(NS - 1, 1)
            finish(NS - 2, 0, full)
            finish(NS - 1, 1, full, LASTP)
            for n in range(2):
                act.wait_ge(s_out[n], 16 * NS // 2)


_INS = ["x", "src", "dst", "edge_type_7", "L0_gnn_weights"]


def kernel(**inputs):
    import numpy as _np
    import concourse.bacc as _bacc
    from concourse import mybir as _mybir
    from concourse.bass_utils import run_bass_kernel_spmd as _run

    nc = _bacc.Bacc("TRN2", target_bir_lowering=False, num_devices=1)
    arrays, args = {}, []
    for name in _INS:
        a = _np.ascontiguousarray(inputs[name])
        arrays[f"in_{name}_dram"] = a
        args.append(nc.dram_tensor(f"in_{name}_dram", a.shape, _mybir.dt.from_np(a.dtype), kind="ExternalInput").ap())
    shape = inputs["x"].shape
    args.append(nc.dram_tensor("out_0_dram", shape, _mybir.dt.float32, kind="ExternalOutput").ap())
    gnn_kernel(nc, *args)
    r = _run(nc, [arrays], core_ids=[0])
    return r.results[0]["out_0_dram"]
```
